# Optimizing a Trainium2 kernel written in Bass

```python
import numpy as np
import jax
import jax.numpy as jnp

def _softmax(x, axis=-1):
    return jax.nn.softmax(x, axis=axis)

def _gelu(x):
    return jax.nn.gelu(x, approximate=True)

def _silu(x):
    return jax.nn.silu(x)

def _sigmoid(x):
    return jax.nn.sigmoid(x)

def _layernorm(x, axis=-1, eps=1e-05):
    m = jnp.mean(x, axis=axis, keepdims=True)
    v = jnp.var(x, axis=axis, keepdims=True)
    return (x - m) / jnp.sqrt(v + eps)

def _scatter_add(tgt, idx, src, axis=0):
    return tgt.at[idx].add(src)

def _segment_sum(src, seg, n):
    return jax.ops.segment_sum(src, seg, n)
kernel_name = 'mk_gnn_preln_d1_gnn_r8_3c7294'

def setup_inputs(seed: int=0):
    np.random.seed(seed)
    _w = jnp.asarray

    def _rec_inputs():
        import jax
        import jax.numpy as jnp
        _gk = jax.random.key(seed)
        x = -0.000202 + 1 * jax.random.normal(jax.random.fold_in(_gk, 1), (12500, 128), jnp.float32)
        src = jax.random.randint(jax.random.fold_in(_gk, 2), (200000,), 0, 12500, jnp.int32)
        dst = jax.random.randint(jax.random.fold_in(_gk, 3), (200000,), 0, 12500, jnp.int32)
        _o = jnp.argsort(dst, stable=True)
        src = src[_o]
        dst = dst[_o]
        edge_attr_128 = -9.77346e-05 + 0.999888 * jax.random.normal(jax.random.fold_in(_gk, 12), (200000, 128), jnp.float32)
        return (x, src, dst, edge_attr_128)
    x, src, dst, edge_attr_128 = _rec_inputs()

    def _L0_gnn_setup():
        import jax, jax.numpy as jnp
        import numpy as np
        N, E = (6250, 50000)
        OBJ_D, REL_D, EFF_D, HID = (128, 128, 128, 256)

        def _mlp_params(key, in_d, hid, out_d, scale=0.02):
            k1, k2 = jax.random.split(key)
            return (jax.random.normal(k1, (in_d, hid), jnp.float32) * scale, jnp.zeros((hid,), jnp.float32), jax.random.normal(k2, (hid, out_d), jnp.float32) * scale, jnp.zeros((out_d,), jnp.float32))

        def _mlp(x, w1, b1, w2, b2):
            h = jax.nn.relu(x @ w1 + b1)
            return h @ w2 + b2
        key = jax.random.key(seed)
        ks = jax.random.split(key, 7)
        objects = jax.random.normal(ks[0], (N, OBJ_D), jnp.float32)
        relations = jax.random.normal(ks[1], (E, REL_D), jnp.float32)
        senders = jax.random.randint(ks[2], (E,), 0, N, jnp.int32)
        receivers = jax.random.randint(ks[3], (E,), 0, N, jnp.int32)
        re_w1, re_b1, re_w2, re_b2 = _mlp_params(ks[4], 2 * OBJ_D + REL_D, HID, EFF_D)
        oe_w1, oe_b1, oe_w2, oe_b2 = _mlp_params(ks[5], OBJ_D, HID, EFF_D)
        ea_w1, ea_b1, ea_w2, ea_b2 = _mlp_params(ks[6], EFF_D + OBJ_D, HID, OBJ_D)
        return dict(objects=objects, relations=relations, senders=senders, receivers=receivers, re_w1=re_w1, re_b1=re_b1, re_w2=re_w2, re_b2=re_b2, oe_w1=oe_w1, oe_b1=oe_b1, oe_w2=oe_w2, oe_b2=oe_b2, ea_w1=ea_w1, ea_b1=ea_b1, ea_w2=ea_w2, ea_b2=ea_b2)
    _L0_gnn_all = _L0_gnn_setup()
    _L0_gnn_in = {k: v for k, v in _L0_gnn_all.items() if k in ('re_w1', 're_b1', 're_w2', 're_b2', 'oe_w1', 'oe_b1', 'oe_w2', 'oe_b2', 'ea_w1', 'ea_b1', 'ea_w2', 'ea_b2')}
    del _L0_gnn_all
    return {'x': x, 'src': src, 'dst': dst, 'edge_attr_128': edge_attr_128, 'L0_gnn_re_w1': _L0_gnn_in['re_w1'], 'L0_gnn_re_b1': _L0_gnn_in['re_b1'], 'L0_gnn_re_w2': _L0_gnn_in['re_w2'], 'L0_gnn_re_b2': _L0_gnn_in['re_b2'], 'L0_gnn_oe_w1': _L0_gnn_in['oe_w1'], 'L0_gnn_oe_b1': _L0_gnn_in['oe_b1'], 'L0_gnn_oe_w2': _L0_gnn_in['oe_w2'], 'L0_gnn_oe_b2': _L0_gnn_in['oe_b2'], 'L0_gnn_ea_w1': _L0_gnn_in['ea_w1'], 'L0_gnn_ea_b1': _L0_gnn_in['ea_b1'], 'L0_gnn_ea_w2': _L0_gnn_in['ea_w2'], 'L0_gnn_ea_b2': _L0_gnn_in['ea_b2']}

def reference(x, src, dst, edge_attr_128, L0_gnn_re_w1, L0_gnn_re_b1, L0_gnn_re_w2, L0_gnn_re_b2, L0_gnn_oe_w1, L0_gnn_oe_b1, L0_gnn_oe_w2, L0_gnn_oe_b2, L0_gnn_ea_w1, L0_gnn_ea_b1, L0_gnn_ea_w2, L0_gnn_ea_b2):
    import jax
    import jax.numpy as jnp

    def _L0_gnn_ref(objects, relations, senders, receivers, re_w1, re_b1, re_w2, re_b2, oe_w1, oe_b1, oe_w2, oe_b2, ea_w1, ea_b1, ea_w2, ea_b2):
        import jax, jax.numpy as jnp
        import numpy as np
        N, E = (6250, 50000)
        OBJ_D, REL_D, EFF_D, HID = (128, 128, 128, 256)

        def _mlp_params(key, in_d, hid, out_d, scale=0.02):
            k1, k2 = jax.random.split(key)
            return (jax.random.normal(k1, (in_d, hid), jnp.float32) * scale, jnp.zeros((hid,), jnp.float32), jax.random.normal(k2, (hid, out_d), jnp.float32) * scale, jnp.zeros((out_d,), jnp.float32))

        def _mlp(x, w1, b1, w2, b2):
            h = jax.nn.relu(x @ w1 + b1)
            return h @ w2 + b2
        _obj_enc = _mlp(objects, oe_w1, oe_b1, oe_w2, oe_b2)
        rel_inputs = jnp.concatenate([objects[senders], objects[receivers], relations], axis=-1)
        rel_effects = _mlp(rel_inputs, re_w1, re_b1, re_w2, re_b2)
        agg_effects = jax.ops.segment_sum(rel_effects, receivers, num_segments=objects.shape[0])
        effect_inputs = jnp.concatenate([objects, agg_effects], axis=-1)
        updated_objects = _mlp(effect_inputs, ea_w1, ea_b1, ea_w2, ea_b2)
        return updated_objects
    h = jnp.maximum(_layernorm(x, axis=-1), 0.0)
    x = x + _L0_gnn_ref(h, edge_attr_128, src, dst, L0_gnn_re_w1, L0_gnn_re_b1, L0_gnn_re_w2, L0_gnn_re_b2, L0_gnn_oe_w1, L0_gnn_oe_b1, L0_gnn_oe_w2, L0_gnn_oe_b2, L0_gnn_ea_w1, L0_gnn_ea_b1, L0_gnn_ea_w2, L0_gnn_ea_b2)
    return x

_drawn_inputs = setup_inputs


def setup_inputs(seed=0):
    import zlib

    import numpy as np

    out = dict(_drawn_inputs(seed))
    spreads = {'L0_gnn_re_b1': (0.0, 0.586),
     'L0_gnn_re_b2': (0.0, 0.1),
     'L0_gnn_oe_b1': (0.0, 0.1),
     'L0_gnn_oe_b2': (0.0, 0.1),
     'L0_gnn_ea_b1': (0.0, 0.375),
     'L0_gnn_ea_b2': (0.0, 0.1)}
    factors = {'edge_attr_128': 6.408}
    for name, (base, spread) in spreads.items():
        noise = np.random.default_rng([zlib.crc32(name.encode()), seed]).standard_normal(out[name].shape)
        drawn = base * np.exp(spread * noise) if base else spread * noise
        out[name] = jnp.asarray(drawn.astype(out[name].dtype))
    for name, factor in factors.items():
        out[name] = (out[name] * factor).astype(out[name].dtype)
    return out
```

```python
import concourse.bass as bass
from concourse import mybir
from contextlib import ExitStack


def bass_gnn_preln_layer_kernel(nc, x, src, dst, edge_attr, re_w1, re_b1, re_w2, re_b2,
                                ea_w1, ea_b1, ea_w2, ea_b2, out):
    f32, f32r = mybir.dt.float32, mybir.dt.float32r
    bf16, i32 = mybir.dt.bfloat16, mybir.dt.int32
    ALU = mybir.AluOpType
    ACT = mybir.ActivationFunctionType
    AX = mybir.AxisListType.X

    L = 128
    N, D = x.shape
    E = src.shape[0]
    HID = re_w1.shape[1]
    EPS = 1e-5

    QUAD = 4
    NQ = -(-N // (QUAD * L))
    NT = NQ * QUAD
    NPAD = NT * L
    FULL = N // L
    REST = N - FULL * L
    XCH = 20
    NXC = NT // XCH
    QPC = XCH // QUAD

    TG = 14
    GE = TG * L
    NG = -(-E // GE)
    TAIL0 = E - GE
    OVER = NG * GE - E
    WIN = L
    PAIRS = TG // 2
    NU = NG * PAIRS
    AW = HID + 2
    DUMMY = NPAD
    NE = -(-E // L)
    GTAIL0 = E - L
    GOVER = NE * L - E
    OUTSIDE = -1000.0
    ZT = 2
    NPRE = 2
    UNROLL = 2 * PAIRS * (NPRE // 2)
    HEAD = PAIRS * 2 + 4
    Q_AT = 4
    ZT = 2
    NPRE = 2
    UNROLL = 2 * PAIRS * (NPRE // 2)
    HEAD = PAIRS * 2 + 4
    Q_AT = 4

    P_dram = nc.dram_tensor("P_dram", [NPAD, HID], f32).ap()
    Q_dram = nc.dram_tensor("Q_dram", [NPAD, HID], f32).ap()
    sums_dram = nc.dram_tensor("sums_dram", [NPAD + L, AW], f32).ap()
    local_dram = nc.dram_tensor("local_dram", [NG, GE], f32).ap()
    local_row_dram = nc.dram_tensor("local_row_dram", [NG, GE], bf16).ap()

    ctx = ExitStack()
    with ctx:
        def sb(name, shape, dt=f32):
            return ctx.enter_context(nc.sbuf_tensor(name, shape, dt))

        def sem(name):
            return ctx.enter_context(nc.semaphore(name))

        bank = [ctx.enter_context(nc.psum_tensor(f"bank{i}", [L, 512], f32)) for i in range(8)]

        w1ab = sb("w1ab", [L, 2 * HID])
        w1c = sb("w1c", [L, HID])
        b1_all = sb("b1_all", [L, HID])
        w2 = sb("w2", [L, 2, D])
        b2_all = sb("b2_all", [L, D])
        u1 = sb("u1", [L, 2, HID])
        c1 = sb("c1", [L, 2])
        u2 = sb("u2", [L, 2, D])
        c2_all = sb("c2_all", [L, D])
        ident = sb("ident", [L, L])
        iota_free = sb("iota_free", [L, L])
        iota_part = sb("iota_part", [L, 1])
        eps_col = sb("eps_col", [L, 1])
        zeros = sb("zeros", [L, 2, AW])

        x_all = sb("x_all", [L, NT, D])
        hT_all = sb("hT_all", [L, NPAD])

        AREA = 66 * 1024
        area = sb("area", [L, AREA // 4])

        class Lay:
            def __init__(self):
                self.at = 0

            def __call__(self, *shape, dt=f32):
                n = 1
                for s in shape:
                    n *= s
                size = {f32: 4, i32: 4, bf16: 2}[dt]
                words = -(-n * size // 4)
                a = area[:, self.at:self.at + words]
                self.at += words
                assert self.at * 4 <= AREA
                if dt != f32:
                    a = a.bitcast(dt)
                if len(shape) == 2:
                    a = a.rearrange("p (a b) -> p a b", a=shape[0])
                if len(shape) == 3:
                    a = a.rearrange("p (a b c) -> p a b c", a=shape[0], b=shape[1])
                return a

        lay0 = Lay()
        recv = lay0(GE, dt=i32)
        local = lay0(GE)
        local_row = lay0(GE, dt=bf16)
        first = lay0(1)
        most = lay0(1)
        least = lay0(1)
        outside = lay0(2)
        ones = lay0(L)
        lay1 = lay0
        stats = lay1(2, QUAD * 6)
        mv = lay1(2, QUAD * 2)
        std = lay1(2, QUAD)
        rstd = lay1(2, QUAD)
        shift = lay1(2, QUAD)
        h_quad = lay1(QUAD, D)
        hT = lay1(QUAD * L)
        P_out = lay1(2, QUAD, HID)
        Q_out = lay1(2, QUAD, HID)
        flag = sb("flag", [L, 1], i32)
        lay2 = Lay()
        e_in = lay2(2, TG, D)
        P_in = lay2(2, TG, HID)
        col = lay2(2, TG)
        row = lay2(2, GE, dt=bf16)
        idx = lay2(4, TG, dt=i32)
        Qw = lay2(2, HID)
        eT = lay2(2, 2 * L)
        pre = lay2(2, 2, HID)
        win = lay2(AW)
        win_out = lay2(2, AW)
        Qhi = sb("Qhi", [L, 2, HID], f32r)
        Qlo = sb("Qlo", [L, 2, HID], f32r)
        ohT = sb("ohT", [L, 2, 2, L], f32r)
        oh = sb("oh", [L, 2, 2, L], f32r)
        hhi = sb("hhi", [L, 2, 2, AW], f32r)
        hlo = sb("hlo", [L, 2, 2, AW], f32r)
        layg = Lay()
        g_src = layg(1, dt=i32)
        g_dst = layg(1, dt=i32)
        g_dst_row = layg(L, dt=i32)
        g_e = layg(D)
        g_P = layg(HID)
        g_Q = layg(HID)
        g_eT = layg(L)
        g_recv = layg(1)
        g_recv_row = layg(L)
        g_same = layg(L)
        g_earlier = layg(L)
        g_count = layg(1)
        g_again = layg(1)
        g_away = layg(1)
        g_row = layg(1, dt=i32)
        g_hidden = layg(HID)
        g_h = layg(AW)
        g_sum = layg(AW)
        below = layg(L)
        all_edges = layg(1)
        new_edges = layg(1)
        dummy_row = layg(1)
        lay3 = Lay()
        S_in = lay3(2, QUAD, AW)
        ST = lay3(2, QUAD * L)
        eff = lay3(QUAD, D)
        effT = lay3(QUAD * L)
        U = lay3(2, QUAD * L)
        xb = lay3(QUAD, D)
        o_out = lay3(2, QUAD, D)

        names = """weights_in ident0 consts zeroed dst_in first_ok local_ok range_ok outside_ok flag_ps flag_ok
            tail_masked row_ok local_st x_pad x_rest_in
            stat_ok agg_ok std_ok rstd_ok shift_ok h_ok hT_ps hT_ok hT_kept P_ps Q_ps P_ok Q_ok
            P_st0 P_st1 Q_st0 Q_st1 zero_st nodes_done
            e_in0 e_in1 col_in0 col_in1 row_in0 row_in1 idx_in0 idx_in1 idx_in2 idx_in3 Q_in0 Q_in1
            Qhi_ok Qlo_ok eT_ps eT_ok pre_ps pre_ok hi_ok lo_ok ohT_ok oh_ok sums_ps win_in win_ok win_st
            fills edges_done
            g_in g_chain_pool g_masks g_rows g_chain g_eT_ps g_eT_ok g_pre_ps g_h_ok g_sum_ps g_sum_ok g_scattered
            S_in0 S_in1 ST_ps ST_ok eff_ps eff_ok effT_ps effT_ok U_ps U_ok o_ps o_ok xb_ok o_st0 o_st1""".split()
        s = type("Sems", (), {n: sem(n) for n in names})
        passed = {e: sem(f"passed_{n}") for n, e in (("pool", nc.gpsimd.engine), ("sp", nc.sync.engine), ("dve", nc.vector.engine))}
        gathered = [[sem(f"gathered{b}_{u}") for u in range(PAIRS)] for b in range(2)]
        x_in = [sem(f"x_in{c}") for c in range(NXC)]
        P_st, Q_st = [s.P_st0, s.P_st1], [s.Q_st0, s.Q_st1]
        e_sem, col_sem, row_sem = [s.e_in0, s.e_in1], [s.col_in0, s.col_in1], [s.row_in0, s.row_in1]
        Q_sem, idx_sem = [s.Q_in0, s.Q_in1], [s.idx_in0, s.idx_in1, s.idx_in2, s.idx_in3]
        S_sem, o_st = [s.S_in0, s.S_in1], [s.o_st0, s.o_st1]

        P_rows = P_dram.rearrange("(q t p) c -> q p t c", t=QUAD, p=L)
        Q_rows = Q_dram.rearrange("(q t p) c -> q p t c", t=QUAD, p=L)
        sum_rows = sums_dram[0:NPAD, :].rearrange("(q t p) c -> q p t c", t=QUAD, p=L)
        out_rows = out[0:FULL * L, :].rearrange("(t p) d -> p t d", p=L)
        x_rows = x[0:FULL * L, :].rearrange("(t p) d -> p t d", p=L)

        class Step:

            def __init__(self, k, turn=None, unroll=0):
                self.k, self.turn, self.unroll = k, turn, unroll
                self.i = k if turn is None else turn * unroll + k

            def back(self, n):
                return Step(self.k - n, self.turn, self.unroll)

            def group(self, size, shift=0):
                return Step((self.k + shift) // size, self.turn, self.unroll // size)

            def uses(self, buffers):
                return self.group(buffers).i + 1

            def within(self, n):
                return self.turn is not None or 0 <= self.k < n

            def least(self, n):
                return self.turn is not None or self.k >= n

            def span(self, size, count=1):
                return bass.ds(self.i * size, count * size)

        class Step:

            def __init__(self, k, turn=None, unroll=0):
                self.k, self.turn, self.unroll = k, turn, unroll
                self.i = k if turn is None else turn * unroll + k

            def back(self, n):
                return Step(self.k - n, self.turn, self.unroll)

            def group(self, size, shift=0):
                return Step((self.k + shift) // size, self.turn, self.unroll // size)

            def uses(self, buffers):
                return self.group(buffers).i + 1

            def within(self, n):
                return self.turn is not None or 0 <= self.k < n

            def least(self, n):
                return self.turn is not None or self.k >= n

            def span(self, size, count=1):
                return bass.ds(self.i * size, count * size)

        def run(eng, n, unroll, head, tail, step):
            loops = max(0, (n - head - tail) // unroll)
            for k in range(head):
                step(Step(k))
            if loops:
                with eng.Fori(0, loops) as turn:
                    for r in range(unroll):
                        step(Step(head + r, turn, unroll))
            for k in range(head + loops * unroll, n):
                step(Step(k))

        def apart(eng):
            eng.sem_inc(passed[eng.engine], 1)

        def either(eng, windowed, general):
            eng.wait_ge(s.flag_ok, 1)
            outsiders = eng.value_load(flag[0:1, 0:1], min_val=0, max_val=2 * NG)
            with eng.If(outsiders > 0):
                general()
            with eng.Else():
                windowed()

        with nc.Block() as block:

            @block.sync
            def _(sp):
                sp.dma_start(recv[0:NG - 1, :], dst[0:(NG - 1) * GE].rearrange("(g e) -> g e", e=GE)).then_inc(s.dst_in, 16)
                sp.dma_start(recv[NG - 1:NG, :], dst[TAIL0:E].rearrange("(g e) -> g e", e=GE)).then_inc(s.dst_in, 16)
                for c in range(NXC):
                    t0, t1 = c * XCH, min((c + 1) * XCH, FULL)
                    sp.dma_start(x_all[:, t0:t1, :], x_rows[:, t0:t1, :]).then_inc(x_in[c], 16)
                    if c == 0:
                        sp.dma_start(w1ab[:, 0:HID], re_w1[0:D, :]).then_inc(s.weights_in, 16)
                        sp.dma_start(w1ab[:, HID:2 * HID], re_w1[D:2 * D, :]).then_inc(s.weights_in, 16)
                        sp.dma_start(w1c[:, :], re_w1[2 * D:3 * D, :]).then_inc(s.weights_in, 16)
                        sp.dma_start(b1_all[:, :], re_b1.partition_broadcast(L)).then_inc(s.weights_in, 16)
                        sp.dma_start(w2[:, :, :], re_w2.rearrange("(k p) n -> p k n", p=L)).then_inc(s.weights_in, 16)
                        sp.dma_start(b2_all[:, :], re_b2.partition_broadcast(L)).then_inc(s.weights_in, 16)
                        sp.dma_start(u1[:, :, :], ea_w1.rearrange("(k p) n -> p k n", p=L)).then_inc(s.weights_in, 16)
                        sp.dma_start(u2[:, :, :], ea_w2.rearrange("(k p) n -> p k n", p=L)).then_inc(s.weights_in, 16)
                        sp.dma_start(c2_all[:, :], ea_b2.partition_broadcast(L)).then_inc(s.weights_in, 16)
                        with nc.allow_non_contiguous_dma(reason="256 biases, two to a partition"):
                            sp.dma_start(c1[:, :], ea_b1.rearrange("(k p) -> p k", p=L)).then_inc(s.weights_in, 16)
                sp.wait_ge(s.x_pad, 1)
                sp.dma_start(x_all[0:REST, FULL, :], x[FULL * L:N, :]).then_inc(s.x_rest_in, 16)

                sp.wait_ge(s.tail_masked, 1)
                sp.dma_start(local_dram, local[0:NG, :]).then_inc(s.local_st, 16)
                sp.wait_ge(s.row_ok, 1)
                sp.dma_start(local_row_dram, local_row[0:NG, :]).then_inc(s.local_st, 16)

                def store_PQ(q):
                    sp.wait_ge(s.P_ok, 2 * (q.i + 1))
                    apart(sp)
                    sp.dma_start(P_rows[q.i] if q.turn is None else P_rows[bass.ds(q.i, 1)].rearrange("o p t c -> (o p) t c"),
                                 P_out[:, q.k % 2, :, :]).then_inc(P_st[q.k % 2], 16)
                    sp.wait_ge(s.Q_ok, 2 * (q.i + 1))
                    apart(sp)
                    sp.dma_start(Q_rows[q.i] if q.turn is None else Q_rows[bass.ds(q.i, 1)].rearrange("o p t c -> (o p) t c"),
                                 Q_out[:, q.k % 2, :, :]).then_inc(Q_st[q.k % 2], 16)

                run(sp, NQ, 2, 1, 0, store_PQ)
                sp.wait_ge(s.zeroed, 1)
                zero_rows = sums_dram.rearrange("(a p) c -> p a c", p=L)
                for a in range(0, NT + 1, ZT):
                    m = min(ZT, NT + 1 - a)
                    sp.dma_start(zero_rows[:, a:a + m, :], zeros[:, 0:m, :]).then_inc(s.zero_st, 16)
                for b in range(2):
                    sp.wait_ge(P_st[b], 16 * ((NQ + 1 - b) // 2))
                    sp.wait_ge(Q_st[b], 16 * ((NQ + 1 - b) // 2))
                sp.wait_ge(s.zero_st, 16 * -(-(NT + 1) // ZT))
                sp.wait_ge(s.local_st, 32)
                sp.wait_ge(s.hT_kept, NQ)
                sp.sem_inc(s.nodes_done, 1)

                def edge_slice(g, size):
                    if g.turn is None:
                        e0 = TAIL0 if g.k == NG - 1 else g.k * GE
                        return slice(e0, e0 + size)
                    return bass.ds(g.i * GE, size)

                def window(g):
                    base = sp.value_load(dst[edge_slice(g, 1)].rearrange("(o n) -> o n", o=1), min_val=0, max_val=N - 1)
                    return bass.ds(base, WIN)

                def load_idx(g):
                    if g.least(4):
                        sp.wait_ge(s.pre_ok, PAIRS * (g.i - 3))
                        apart(sp)
                    sp.dma_start(idx[:, g.k % 4, :], src[edge_slice(g, GE)].rearrange("(p t) -> p t", t=TG)).then_inc(idx_sem[g.k % 4], 16)

                def group_step(g):
                    b = g.k % 2
                    if g.back(-1).within(NG):
                        load_idx(g.back(-1))
                    if g.within(NG):
                        rows = window(g)
                        if g.least(2):
                            sp.wait_ge(s.ohT_ok, PAIRS * (g.i - 1))
                            apart(sp)
                            sp.wait_ge(s.oh_ok, PAIRS * (g.i - 1))
                            apart(sp)
                            sp.wait_ge(s.Qlo_ok, g.i - 1)
                            apart(sp)
                            sp.wait_ge(s.eT_ps, PAIRS * (g.i - 1))
                            apart(sp)
                        sp.dma_start(row[:, b, :], local_row_dram[bass.ds(g.i, 1), :].rearrange("o e -> (o e)").partition_broadcast(L)).then_inc(row_sem[b], 16)
                        sp.dma_start(col[:, b, :], local_dram[bass.ds(g.i, 1), :].rearrange("o (p t) -> (o p) t", t=TG)).then_inc(col_sem[b], 16)
                        sp.dma_start(Qw[:, b, :], Q_dram[rows, :]).then_inc(Q_sem[b], 16)
                        sp.dma_start(e_in[:, b, :, :], edge_attr[edge_slice(g, GE), :].rearrange("(p t) d -> p t d", t=TG)).then_inc(e_sem[b], 16)
                    j = g.back(2)
                    if j.least(0):
                        sp.wait_ge(s.win_ok, j.i + 1)
                        apart(sp)
                        sp.dma_start(sums_dram[window(j), :], win_out[:, j.k % 2, :]).then_inc(s.win_st, 16)
                        if j.back(-1).within(NG):
                            load_window(j.back(-1))

                def load_window(j):
                    rows = window(j)
                    if j.least(1):
                        sp.wait_ge(s.win_st, 16 * j.i)
                        apart(sp)
                    sp.dma_start(win[:, :], sums_dram[rows, :]).then_inc(s.win_in, 16)

                def windowed():
                    load_idx(Step(0))
                    load_window(Step(0))
                    run(sp, NG + 2, 4, 4, 4, group_step)
                    sp.wait_ge(s.win_st, 16 * NG)

                def general():
                    def tile_step(i):
                        if i.least(1):
                            sp.wait_ge(s.g_scattered, 16 * i.i)
                            apart(sp)
                        e = bass.ds(i.i * L, L) if i.turn is not None or i.k < NE - 1 else bass.ds(GTAIL0, L)
                        sp.dma_start(g_src[:, :], src[e].rearrange("(p o) -> p o", o=1)).then_inc(s.g_in, 16)
                        sp.dma_start(g_dst[:, :], dst[e].rearrange("(p o) -> p o", o=1)).then_inc(s.g_in, 16)
                        sp.dma_start(g_dst_row[:, :], dst[e].partition_broadcast(L)).then_inc(s.g_in, 16)
                        sp.dma_start(g_e[:, :], edge_attr[e, :]).then_inc(s.g_in, 16)

                    run(sp, NE, 1, 1, 1, tile_step)
                    sp.wait_ge(s.g_scattered, 16 * NE)

                either(sp, windowed, general)
                sp.sem_inc(s.edges_done, 1)

                def move(q):
                    if q.within(NQ):
                        if q.least(2):
                            sp.wait_ge(s.eff_ok, QUAD * (q.i - 1))
                            apart(sp)
                            sp.wait_ge(s.ST_ps, q.i - 1)
                            apart(sp)
                        sp.dma_start(S_in[:, q.k % 2, :, :], sum_rows[bass.ds(q.i, 1)].rearrange("o p t c -> (o p) t c")).then_inc(S_sem[q.k % 2], 16)
                    j = q.back(4)
                    if j.least(0):
                        sp.wait_ge(s.o_ok, j.i + 1)
                        apart(sp)
                        b = j.k % 2
                        have = QUAD if j.turn is not None else min(QUAD, FULL - j.k * QUAD)
                        if have:
                            sp.dma_start(out_rows[:, bass.ds(j.i * QUAD, have), :], o_out[:, b, 0:have, :]).then_inc(o_st[b], 16)
                        if have < QUAD:
                            sp.dma_start(out[FULL * L:N, :], o_out[0:REST, b, have, :]).then_inc(o_st[b], 16)

                run(sp, NQ + 4, 2, 4, 4, move)
                last = (NQ - 1) % 2
                sp.wait_ge(o_st[1 - last], 16 * (NQ // 2))
                sp.wait_ge(o_st[last], 16 * ((NQ + 1) // 2 + (1 if FULL > (NQ - 1) * QUAD else 0)))

            @block.gpsimd
            def _(pool):
                nc.gpsimd.memset(x_all[:, FULL:NT, :], 0.0).then_inc(s.x_pad, 1)
                nc.gpsimd.memset(ident[:], 0.0).then_inc(s.ident0, 1)
                nc.gpsimd.memset(eps_col[:], EPS).then_inc(s.consts, 1)
                nc.gpsimd.memset(ones[:], 1.0).then_inc(s.consts, 1)
                pool.wait_ge(s.ident0, 1)
                nc.gpsimd.affine_select(out=ident[:], in_=ident[:], compare_op=ALU.not_equal, fill=1.0, base=0,
                                        pattern=[[-1, L]], channel_multiplier=1).then_inc(s.consts, 1)
                nc.gpsimd.iota(iota_free[:], pattern=[[1, L]], base=0, channel_multiplier=0,
                               allow_small_or_imprecise_dtypes=True).then_inc(s.consts, 1)
                nc.gpsimd.iota(iota_part[:], pattern=[[0, 1]], base=0, channel_multiplier=1,
                               allow_small_or_imprecise_dtypes=True).then_inc(s.consts, 1)
                nc.gpsimd.memset(zeros[:], 0.0).then_inc(s.zeroed, 1)
                pool.wait_ge(s.range_ok, 2)
                pool.wait_ge(s.consts, 5)
                pool.wait_ge(s.zeroed, 1)
                q0 = (NG - 1) // 32 * 32
                nc.gpsimd.affine_select(out=local[q0:NG, 0:OVER], in_=local[q0:NG, 0:OVER], compare_op=ALU.not_equal,
                                        fill=OUTSIDE, base=q0 - (NG - 1), pattern=[[0, OVER]],
                                        channel_multiplier=1).then_inc(s.tail_masked, 1)

                def keep(q):
                    pool.wait_ge(s.hT_ok, q.i + 1)
                    nc.gpsimd.tensor_copy(hT_all[:, q.span(QUAD * L)], hT[:, :]).then_inc(s.hT_kept, 1)

                run(pool, NQ, 1, 1, 0, keep)

                pool.wait_ge(s.nodes_done, 1)

                def gather(g):
                    b = g.k % 2
                    pool.wait_ge(idx_sem[g.k % 4], 16 * g.uses(4))
                    apart(pool)
                    for u in range(PAIRS):
                        if g.least(2):
                            pool.wait_ge(s.pre_ok, PAIRS * (g.i - 2) + u + 1)
                            apart(pool)
                        for t in (2 * u, 2 * u + 1):
                            nc.gpsimd.indirect_dma_start(
                                out=P_in[:, b, t, :], out_offset=None, in_=P_dram[:, :],
                                in_offset=bass.IndirectOffsetOnAxis(ap=idx[:, g.k % 4, t:t + 1], axis=0)
                            ).then_inc(gathered[b][u], 16)

                def general():
                    nc.gpsimd.memset(below[:], 1.0).then_inc(s.g_chain_pool, 1)
                    nc.gpsimd.memset(all_edges[:], 1.0).then_inc(s.g_masks, 1)
                    nc.gpsimd.memset(new_edges[:], 1.0).then_inc(s.g_chain_pool, 1)
                    nc.gpsimd.iota(dummy_row[:], pattern=[[0, 1]], base=DUMMY, channel_multiplier=1,
                                   allow_small_or_imprecise_dtypes=True).then_inc(s.g_masks, 1)
                    pool.wait_ge(s.g_chain_pool, 2)
                    nc.gpsimd.affine_select(out=below[:], in_=below[:], compare_op=ALU.is_ge, fill=0.0, base=-1,
                                            pattern=[[-1, L]], channel_multiplier=1).then_inc(s.g_masks, 1)
                    nc.gpsimd.affine_select(out=new_edges[:], in_=new_edges[:], compare_op=ALU.is_ge, fill=0.0, base=-GOVER,
                                            pattern=[[0, 1]], channel_multiplier=1).then_inc(s.g_masks, 1)

                    def tile_step(i):
                        pool.wait_ge(s.g_in, 64 * (i.i + 1))
                        apart(pool)
                        for rows, table, index in ((g_P, P_dram, g_src), (g_Q, Q_dram, g_dst)):
                            nc.gpsimd.indirect_dma_start(
                                out=rows[:, :], out_offset=None, in_=table[:, :],
                                in_offset=bass.IndirectOffsetOnAxis(ap=index[:, 0:1], axis=0)).then_inc(s.g_rows, 16)
                        pool.wait_ge(s.g_sum_ok, i.i + 1)
                        apart(pool)
                        nc.gpsimd.indirect_dma_start(
                            out=sums_dram[:, :], out_offset=bass.IndirectOffsetOnAxis(ap=g_row[:, 0:1], axis=0),
                            in_=g_sum[:, :], in_offset=None, compute_op=ALU.add).then_inc(s.g_scattered, 16)

                    run(pool, NE, 1, 1, 1, tile_step)

                either(pool, lambda: run(pool, NG, 4, 2, 0, gather), general)

                pool.wait_ge(s.edges_done, 1)

                def add_bias(q):
                    if q.least(1):
                        pool.wait_ge(s.o_ok, q.i)
                    nc.gpsimd.tensor_tensor(xb[:, :, :], x_all[:, q.span(QUAD), :],
                                            c2_all[:, :].unsqueeze(1).to_broadcast([L, QUAD, D]), ALU.add).then_inc(s.xb_ok, 1)

                run(pool, NQ, 1, 1, 0, add_bias)

            @block.scalar
            def _(act):
                act.wait_ge(s.consts, 5)
                act.wait_ge(s.weights_in, 160)

                def take_std(q):
                    act.wait_ge(s.agg_ok, QUAD * (q.i + 1))
                    if q.least(2):
                        act.wait_ge(s.rstd_ok, q.i - 1)
                    b = q.k % 2
                    nc.scalar.activation(std[:, b, :], mv[:, b, :].rearrange("p (t c) -> p t c", c=2)[:, :, 1],
                                         ACT.Sqrt, bias=eps_col[:, 0:1]).then_inc(s.std_ok, 1)

                def normalise(q):
                    act.wait_ge(s.shift_ok, q.i + 1)
                    if q.least(1):
                        act.wait_ge(s.hT_ps, q.i)
                    for t in range(QUAD):
                        h = nc.scalar.activation(h_quad[:, t, :], x_all[:, bass.ds(q.i * QUAD + t, 1), :].rearrange("p o d -> p (o d)"),
                                                 ACT.Relu, bias=shift[:, q.k % 2, t:t + 1], scale=rstd[:, q.k % 2, t:t + 1])
                    h.then_inc(s.h_ok, 1)

                take_std(Step(0))
                normalise(Step(0))
                take_std(Step(1))

                def node_step(q):
                    if q.within(NQ):
                        act.wait_ge(s.hT_ps, q.i + 1)
                        if q.least(1):
                            act.wait_ge(s.Q_ps, 2 * q.i)
                            act.wait_ge(s.hT_kept, q.i)
                        nc.scalar.copy(hT[:, :], bank[0][:, :]).then_inc(s.hT_ok, 1)
                    if q.back(-1).within(NQ):
                        normalise(q.back(-1))
                    if q.back(-2).within(NQ):
                        take_std(q.back(-2))
                    p = q.back(1)
                    if p.least(0):
                        if p.least(2):
                            act.wait_ge(P_st[p.k % 2], 16 * (p.uses(2) - 1))
                        for half in range(2):
                            act.wait_ge(s.P_ps, 2 * p.i + half + 1)
                            nc.scalar.copy(P_out[:, p.k % 2, 2 * half:2 * half + 2, :],
                                           bank[1 + half][:, :].rearrange("p (t c) -> p t c", t=2)).then_inc(s.P_ok, 1)

                run(act, NQ + 1, 2, 3, 3, node_step)

                act.wait_ge(s.nodes_done, 1)

                def q_hi(g):
                    act.wait_ge(Q_sem[g.k % 2], 16 * g.uses(2))
                    if g.least(2):
                        act.wait_ge(s.pre_ps, PAIRS * (g.i - 1))
                    nc.scalar.copy(Qhi[:, g.k % 2, :], Qw[:, g.k % 2, :]).then_inc(s.Qhi_ok, 1)

                def edge_step(u):
                    if u.within(NU):
                        act.wait_ge(s.eT_ps, u.i + 1)
                        if u.least(2):
                            act.wait_ge(s.pre_ps, u.i - 1)
                        nc.scalar.copy(eT[:, u.k % 2, :], bank[u.k % 2][:, 0:2 * L]).then_inc(s.eT_ok, 1)
                    v = u.back(2)
                    if v.within(NU):
                        act.wait_ge(s.pre_ok, v.i + 1)
                        if v.least(2):
                            act.wait_ge(s.sums_ps, v.i - 1)
                        nc.scalar.activation(hhi[:, v.k % 2, :, 0:HID], pre[:, v.k % 2, :, :], ACT.Relu).then_inc(s.hi_ok, 1)
                    if u.k % PAIRS == Q_AT and u.group(PAIRS, PAIRS - Q_AT).within(NG):
                        q_hi(u.group(PAIRS, PAIRS - Q_AT))

                def windowed():
                    q_hi(Step(0))
                    run(act, NU + 4, UNROLL, HEAD, PAIRS, edge_step)

                def general():
                    def tile_step(i):
                        act.wait_ge(s.g_eT_ps, i.i + 1)
                        nc.scalar.copy(g_eT[:, :], bank[0][:, 0:L]).then_inc(s.g_eT_ok, 1)

                    run(act, NE, 1, 1, 1, tile_step)

                either(act, windowed, general)

                act.wait_ge(s.edges_done, 1)

                def update_step(q):
                    if q.within(NQ):
                        act.wait_ge(s.ST_ps, q.i + 1)
                        if q.least(1):
                            act.wait_ge(s.eff_ps, q.i)
                        nc.scalar.copy(ST[:, 0, :], bank[0][:, :]).then_inc(s.ST_ok, 1)
                    p = q.back(2)
                    if p.within(NQ):
                        act.wait_ge(s.effT_ps, p.i + 1)
                        if p.least(1):
                            act.wait_ge(s.U_ps, 2 * p.i)
                        nc.scalar.copy(effT[:, :], bank[3][:, :]).then_inc(s.effT_ok, 1)
                    p = q.back(3)
                    if p.within(NQ):
                        for k in range(2):
                            act.wait_ge(s.U_ps, 2 * p.i + k + 1)
                            if k == 0 and p.least(1):
                                act.wait_ge(s.o_ps, p.i)
                            nc.scalar.activation(U[:, k, :], bank[4 + k][:, :], ACT.Relu, bias=c1[:, k:k + 1]).then_inc(s.U_ok, 1)

                run(act, NQ + 4, 1, 4, 4, update_step)

            @block.vector
            def _(dve):
                nc.vector.memset(outside[:], 0.0).then_inc(s.first_ok, 1)
                nc.vector.memset(hhi[:, :, :, HID:AW].bitcast(f32), 1.0).then_inc(s.fills, 1)
                nc.vector.memset(hlo[:, :, :, HID:AW].bitcast(f32), 0.0).then_inc(s.fills, 1)
                dve.wait_ge(s.dst_in, 32)
                nc.vector.tensor_copy(first[0:NG, :], recv[0:NG, 0:1]).then_inc(s.first_ok, 1)
                dve.wait_ge(s.first_ok, 2)
                nc.vector.tensor_scalar(local[0:NG, :], recv[0:NG, :], first[0:NG, 0:1], None, ALU.subtract).then_inc(s.local_ok, 1)
                dve.wait_ge(s.local_ok, 1)
                nc.vector.tensor_reduce(most[0:NG, :], local[0:NG, :], AX, ALU.max).then_inc(s.range_ok, 1)
                nc.vector.tensor_reduce(least[0:NG, :], local[0:NG, :], AX, ALU.min).then_inc(s.range_ok, 1)
                dve.wait_ge(s.range_ok, 2)
                nc.vector.tensor_scalar(outside[0:NG, 0:1], most[0:NG, :], float(WIN - 1), None, ALU.is_gt).then_inc(s.outside_ok, 1)
                nc.vector.tensor_scalar(outside[0:NG, 1:2], least[0:NG, :], 0.0, None, ALU.is_lt).then_inc(s.outside_ok, 1)
                dve.wait_ge(s.tail_masked, 1)
                nc.vector.tensor_copy(local_row[0:NG, :].rearrange("g (t p) -> g p t", p=L),
                                      local[0:NG, :].rearrange("g (p t) -> g p t", t=TG)).then_inc(s.row_ok, 1)
                dve.wait_ge(s.flag_ps, 1)
                nc.vector.tensor_copy(flag[:, :], bank[7][:, 0:1]).then_inc(s.flag_ok, 1)
                dve.wait_ge(s.weights_in, 160)

                def take_stats(q):
                    b = q.k % 2
                    if q.least(2):
                        dve.wait_ge(s.std_ok, q.i - 1)
                        dve.wait_ge(s.shift_ok, q.i - 1)
                    for t in range(QUAD):
                        nc.vector.bn_stats(stats[:, b, 6 * t:6 * t + 6],
                                           x_all[:, bass.ds(q.i * QUAD + t, 1), :].rearrange("p o d -> p (o d)")).then_inc(s.stat_ok, 1)
                    for t in range(QUAD):
                        dve.wait_ge(s.stat_ok, QUAD * q.i + t + 1)
                        apart(dve)
                        nc.vector.bn_aggr(mv[:, b, 2 * t:2 * t + 2], stats[:, b, 6 * t:6 * t + 6]).then_inc(s.agg_ok, 1)

                def take_rstd(q):
                    b = q.k % 2
                    dve.wait_ge(s.std_ok, q.i + 1)
                    if q.least(2):
                        dve.wait_ge(s.h_ok, q.i - 1)
                    nc.vector.reciprocal(rstd[:, b, :], std[:, b, :]).then_inc(s.rstd_ok, 1)
                    dve.wait_ge(s.rstd_ok, q.i + 1)
                    nc.vector.scalar_tensor_tensor(shift[:, b, :], mv[:, b, :].rearrange("p (t c) -> p t c", c=2)[:, :, 0],
                                                   -1.0, rstd[:, b, :], ALU.mult, ALU.mult).then_inc(s.shift_ok, 1)

                dve.wait_ge(x_in[0], 16)
                take_stats(Step(0))
                take_rstd(Step(0))
                take_stats(Step(1))

                for c in range(1, NXC):
                    dve.wait_ge(x_in[c], 16)
                dve.wait_ge(s.x_rest_in, 16)

                def node_step(q):
                    if q.back(-1).within(NQ):
                        take_rstd(q.back(-1))
                    if q.back(-2).within(NQ):
                        take_stats(q.back(-2))
                    p = q.back(1)
                    if p.least(0):
                        if p.least(2):
                            dve.wait_ge(Q_st[p.k % 2], 16 * (p.uses(2) - 1))
                        for half in range(2):
                            dve.wait_ge(s.Q_ps, 2 * p.i + half + 1)
                            nc.vector.tensor_tensor(Q_out[:, p.k % 2, 2 * half:2 * half + 2, :],
                                                    bank[3 + half][:, :].rearrange("p (t c) -> p t c", t=2),
                                                    b1_all[:, :].unsqueeze(1).to_broadcast([L, 2, HID]), ALU.add).then_inc(s.Q_ok, 1)

                run(dve, NQ + 1, 2, 3, 3, node_step)

                dve.wait_ge(s.nodes_done, 1)

                def q_lo(g):
                    b = g.k % 2
                    dve.wait_ge(s.Qhi_ok, g.i + 1)
                    if g.least(2):
                        dve.wait_ge(s.pre_ps, PAIRS * (g.i - 1))
                    nc.vector.tensor_tensor(Qlo[:, b, :], Qw[:, b, :], Qhi[:, b, :].bitcast(f32), ALU.subtract).then_inc(s.Qlo_ok, 1)

                def edge_step(u):
                    v = u.back(2)
                    if v.within(NU):
                        g, b, at = v.group(PAIRS), v.k % 2, v.k % PAIRS
                        dve.wait_ge(s.pre_ps, v.i + 1)
                        dve.wait_ge(gathered[g.k % 2][at], 32 * g.uses(2))
                        if v.least(2):
                            dve.wait_ge(s.lo_ok, v.i - 1)
                        nc.vector.tensor_tensor(pre[:, b, :, :], bank[2 + v.k % NPRE][:, :].rearrange("p (t c) -> p t c", t=2),
                                                P_in[:, g.k % 2, 2 * at:2 * at + 2, :], ALU.add).then_inc(s.pre_ok, 1)
                    w = u.back(3)
                    if w.within(NU):
                        b = w.k % 2
                        dve.wait_ge(s.hi_ok, w.i + 1)
                        if w.least(2):
                            dve.wait_ge(s.sums_ps, w.i - 1)
                        nc.vector.scalar_tensor_tensor(hlo[:, b, :, 0:HID], pre[:, b, :, :], 0.0,
                                                       hhi[:, b, :, 0:HID].bitcast(f32), ALU.max, ALU.subtract).then_inc(s.lo_ok, 1)
                    if u.within(NU):
                        g, at = u.group(PAIRS), u.k % PAIRS
                        if at == 0:
                            dve.wait_ge(row_sem[g.k % 2], 16 * g.uses(2))
                        if u.least(2):
                            dve.wait_ge(s.pre_ps, u.i - 1)
                        nc.vector.tensor_scalar(ohT[:, u.k % 2, :, :].rearrange("p t e -> p (t e)"),
                                                row[:, g.k % 2, 2 * L * at:2 * L * (at + 1)], iota_part[:, 0:1], None,
                                                ALU.is_equal).then_inc(s.ohT_ok, 1)
                    if v.within(NU):
                        g, at = v.group(PAIRS), v.k % PAIRS
                        if at == 0:
                            dve.wait_ge(col_sem[g.k % 2], 16 * g.uses(2))
                        if v.least(2):
                            dve.wait_ge(s.sums_ps, v.i - 1)
                        nc.vector.tensor_tensor(oh[:, v.k % 2, :, :], iota_free[:, :].unsqueeze(1).to_broadcast([L, 2, L]),
                                                col[:, g.k % 2, 2 * at:2 * at + 2].unsqueeze(2).to_broadcast([L, 2, L]),
                                                ALU.is_equal).then_inc(s.oh_ok, 1)
                    if u.k % PAIRS == Q_AT + 1 and u.group(PAIRS, PAIRS - Q_AT - 1).within(NG):
                        q_lo(u.group(PAIRS, PAIRS - Q_AT - 1))
                    g = u.group(PAIRS, -PAIRS - 3)
                    if u.k % PAIRS == 3 and g.within(NG):
                        dve.wait_ge(s.sums_ps, PAIRS * (g.i + 1))
                        dve.wait_ge(s.win_in, 16 * (g.i + 1))
                        if g.least(2):
                            dve.wait_ge(s.win_st, 16 * (g.i - 1))
                        nc.vector.tensor_tensor(win_out[:, g.k % 2, :], bank[6 + g.k % 2][:, 0:AW], win[:, :], ALU.add).then_inc(s.win_ok, 1)

                def windowed():
                    q_lo(Step(0))
                    run(dve, NU + 4, UNROLL, HEAD, PAIRS, edge_step)

                def general():
                    dve.wait_ge(s.g_masks, 4)
                    LINKS = 11

                    def tile_step(i):
                        linked = [0]

                        def link(ins):
                            linked[0] += 1
                            ins.then_inc(s.g_chain, 1)
                            dve.wait_ge(s.g_chain, i.i * LINKS + linked[0])

                        dve.wait_ge(s.g_in, 64 * (i.i + 1))
                        link(nc.vector.tensor_copy(g_recv[:, :], g_dst[:, :]))
                        link(nc.vector.tensor_copy(g_recv_row[:, :], g_dst_row[:, :]))
                        link(nc.vector.tensor_scalar(g_same[:, :], g_recv_row[:, :], g_recv[:, 0:1], None, ALU.is_equal))
                        link(nc.vector.tensor_tensor(g_earlier[:, :], g_same[:, :], below[:, :], ALU.mult))
                        link(nc.vector.tensor_reduce(g_count[:, :], g_earlier[:, :], AX, ALU.add))
                        link(nc.vector.tensor_scalar(g_again[:, :], g_count[:, :], 1.0, None, ALU.min))
                        link(nc.vector.tensor_tensor(g_away[:, :], dummy_row[:, :], g_recv[:, :], ALU.subtract))
                        link(nc.vector.scalar_tensor_tensor(g_row[:, :], g_away[:, :], g_again[:, 0:1], g_recv[:, :],
                                                            ALU.mult, ALU.add))
                        real = all_edges if i.turn is not None or i.k < NE - 1 else new_edges
                        dve.wait_ge(s.g_pre_ps, i.i + 1)
                        dve.wait_ge(s.g_rows, 32 * (i.i + 1))
                        link(nc.vector.tensor_tensor(g_hidden[:, :], bank[1][:, 0:HID], g_P[:, :], ALU.add))
                        link(nc.vector.tensor_tensor(g_hidden[:, :], g_hidden[:, :], g_Q[:, :], ALU.add))
                        link(nc.vector.tensor_copy(g_h[:, HID:AW], real[:, 0:1].to_broadcast([L, 2])))
                        nc.vector.tensor_scalar(g_h[:, 0:HID], g_hidden[:, :], 0.0, real[:, 0:1], ALU.max, ALU.mult).then_inc(s.g_h_ok, 1)
                        dve.wait_ge(s.g_sum_ps, i.i + 1)
                        nc.vector.tensor_copy(g_sum[:, :], bank[2][:, 0:AW]).then_inc(s.g_sum_ok, 1)

                    run(dve, NE, 1, 1, 1, tile_step)

                either(dve, windowed, general)

                dve.wait_ge(s.edges_done, 1)

                def update_step(q):
                    if q.within(NQ):
                        dve.wait_ge(s.ST_ps, q.i + 1)
                        if q.least(1):
                            dve.wait_ge(s.eff_ps, q.i)
                        nc.vector.tensor_copy(ST[:, 1, :], bank[1][:, :]).then_inc(s.ST_ok, 1)
                    p = q.back(1)
                    if p.within(NQ):
                        dve.wait_ge(s.eff_ps, p.i + 1)
                        if p.least(1):
                            dve.wait_ge(s.effT_ps, p.i)
                        for t in range(QUAD):
                            nc.vector.scalar_tensor_tensor(eff[:, t, :], b2_all[:, :], S_in[:, p.k % 2, t, HID:HID + 1],
                                                           bank[2][:, t * D:(t + 1) * D], ALU.mult, ALU.add).then_inc(s.eff_ok, 1)
                    p = q.back(4)
                    if p.within(NQ):
                        dve.wait_ge(s.o_ps, p.i + 1)
                        dve.wait_ge(s.xb_ok, p.i + 1)
                        if p.least(2):
                            dve.wait_ge(o_st[p.k % 2], 16 * (p.uses(2) - 1))
                        nc.vector.tensor_tensor(o_out[:, p.k % 2, :, :], bank[6][:, :].rearrange("p (t d) -> p t d", t=QUAD),
                                                xb[:, :, :], ALU.add).then_inc(s.o_ok, 1)

                run(dve, NQ + 4, 2, 6, 4, update_step)

            @block.tensor
            def _(pe):
                pe.wait_ge(s.consts, 5)
                pe.wait_ge(s.outside_ok, 2)
                nc.tensor.matmul(bank[7][:, 0:1], ones[:, :], outside[:, 0:1], start=True, stop=False)
                nc.tensor.matmul(bank[7][:, 0:1], ones[:, :], outside[:, 1:2], start=False, stop=True).then_inc(s.flag_ps, 1)
                pe.wait_ge(s.weights_in, 160)

                def node_step(q):
                    if q.within(NQ):
                        pe.wait_ge(s.h_ok, q.i + 1)
                        if q.least(1):
                            pe.wait_ge(s.hT_ok, q.i)
                        for t in range(QUAD):
                            mm = nc.tensor.transpose(bank[0][:, t * L:(t + 1) * L], h_quad[:, t, :], ident[:, :])
                        mm.then_inc(s.hT_ps, 1)
                    p = q.back(1)
                    if p.least(0):
                        pe.wait_ge(s.hT_ok, p.i + 1)
                        for half in range(2):
                            for m, (made, taken) in enumerate(((s.P_ps, s.P_ok), (s.Q_ps, s.Q_ok))):
                                if p.least(1):
                                    pe.wait_ge(taken, 2 * (p.i - 1) + half + 1)
                                for t in (2 * half, 2 * half + 1):
                                    mm = nc.tensor.matmul(bank[1 + 2 * m + half][:, t % 2 * HID:(t % 2 + 1) * HID],
                                                          hT[:, t * L:(t + 1) * L], w1ab[:, m * HID:(m + 1) * HID], start=True, stop=True)
                                mm.then_inc(made, 1)

                run(pe, NQ + 1, 1, 2, 1, node_step)

                pe.wait_ge(s.nodes_done, 1)

                def edge_step(u):
                    if u.within(NU):
                        g, at = u.group(PAIRS), u.k % PAIRS
                        if at == 0:
                            pe.wait_ge(e_sem[g.k % 2], 16 * g.uses(2))
                        if u.least(2):
                            pe.wait_ge(s.eT_ok, u.i - 1)
                        for t in range(2):
                            mm = nc.tensor.transpose(bank[u.k % 2][:, t * L:(t + 1) * L], e_in[:, g.k % 2, 2 * at + t, :], ident[:, :])
                        mm.then_inc(s.eT_ps, 1)
                    v = u.back(1)
                    if v.within(NU):
                        g, b = v.group(PAIRS), v.k % 2
                        pe.wait_ge(s.eT_ok, v.i + 1)
                        pe.wait_ge(s.ohT_ok, v.i + 1)
                        if v.k % PAIRS == 0:
                            pe.wait_ge(s.Qlo_ok, g.i + 1)
                        if v.least(NPRE):
                            pe.wait_ge(s.pre_ok, v.i - NPRE + 1)
                        for t in range(2):
                            o = bank[2 + v.k % NPRE][:, t * HID:(t + 1) * HID]
                            nc.tensor.matmul(o, eT[:, b, t * L:(t + 1) * L], w1c[:, :], start=True, stop=False)
                            nc.tensor.matmul(o, ohT[:, b, t, :], Qhi[:, g.k % 2, :], start=False, stop=False)
                            mm = nc.tensor.matmul(o, ohT[:, b, t, :], Qlo[:, g.k % 2, :], start=False, stop=True)
                        mm.then_inc(s.pre_ps, 1)
                    w = u.back(3)
                    if w.within(NU):
                        g, at, b = w.group(PAIRS), w.k % PAIRS, w.k % 2
                        pe.wait_ge(s.lo_ok, w.i + 1)
                        pe.wait_ge(s.oh_ok, w.i + 1)
                        if at == 0 and g.least(2):
                            pe.wait_ge(s.win_ok, g.i - 1)
                        for t in range(2):
                            o = bank[6 + g.k % 2][:, 0:AW]
                            nc.tensor.matmul(o, oh[:, b, t, :], hhi[:, b, t, :], start=(at == 0 and t == 0), stop=False)
                            mm = nc.tensor.matmul(o, oh[:, b, t, :], hlo[:, b, t, :], start=False, stop=(at == PAIRS - 1 and t == 1))
                        mm.then_inc(s.sums_ps, 1)

                def windowed():
                    pe.wait_ge(s.fills, 2)
                    run(pe, NU + 4, UNROLL, HEAD, PAIRS, edge_step)

                def general():
                    def tile_step(i):
                        pe.wait_ge(s.g_in, 64 * (i.i + 1))
                        nc.tensor.transpose(bank[0][:, 0:L], g_e[:, :], ident[:, :]).then_inc(s.g_eT_ps, 1)
                        pe.wait_ge(s.g_eT_ok, i.i + 1)
                        nc.tensor.matmul(bank[1][:, 0:HID], g_eT[:, :], w1c[:, :], start=True, stop=True).then_inc(s.g_pre_ps, 1)
                        pe.wait_ge(s.g_h_ok, i.i + 1)
                        nc.tensor.matmul(bank[2][:, 0:AW], g_same[:, :], g_h[:, :], start=True, stop=True).then_inc(s.g_sum_ps, 1)

                    run(pe, NE, 1, 1, 1, tile_step)

                either(pe, windowed, general)

                pe.wait_ge(s.edges_done, 1)

                def update_step(q):
                    if q.within(NQ):
                        b = q.k % 2
                        pe.wait_ge(S_sem[b], 16 * q.uses(2))
                        if q.least(1):
                            pe.wait_ge(s.ST_ok, 2 * q.i)
                        for k in range(2):
                            for t in range(QUAD):
                                mm = nc.tensor.transpose(bank[k][:, t * L:(t + 1) * L], S_in[:, b, t, k * L:(k + 1) * L], ident[:, :])
                        mm.then_inc(s.ST_ps, 1)
                    p = q.back(1)
                    if p.within(NQ):
                        pe.wait_ge(s.ST_ok, 2 * (p.i + 1))
                        if p.least(1):
                            pe.wait_ge(s.eff_ok, QUAD * p.i)
                        for t in range(QUAD):
                            for k in range(2):
                                mm = nc.tensor.matmul(bank[2][:, t * D:(t + 1) * D], ST[:, k, t * L:(t + 1) * L], w2[:, k, :],
                                                      start=(k == 0), stop=(k == 1))
                        mm.then_inc(s.eff_ps, 1)
                    p = q.back(2)
                    if p.within(NQ):
                        pe.wait_ge(s.eff_ok, QUAD * (p.i + 1))
                        if p.least(1):
                            pe.wait_ge(s.effT_ok, p.i)
                        for t in range(QUAD):
                            mm = nc.tensor.transpose(bank[3][:, t * L:(t + 1) * L], eff[:, t, :], ident[:, :])
                        mm.then_inc(s.effT_ps, 1)
                    p = q.back(3)
                    if p.within(NQ):
                        pe.wait_ge(s.effT_ok, p.i + 1)
                        for k in range(2):
                            if p.least(1):
                                pe.wait_ge(s.U_ok, 2 * (p.i - 1) + k + 1)
                            nc.tensor.matmul(bank[4 + k][:, :], u1[:, 0, k * L:(k + 1) * L], hT_all[:, p.span(QUAD * L)], start=True, stop=False)
                            nc.tensor.matmul(bank[4 + k][:, :], u1[:, 1, k * L:(k + 1) * L], effT[:, :], start=False, stop=True).then_inc(s.U_ps, 1)
                    p = q.back(4)
                    if p.within(NQ):
                        pe.wait_ge(s.U_ok, 2 * (p.i + 1))
                        if p.least(1):
                            pe.wait_ge(s.o_ok, p.i)
                        for t in range(QUAD):
                            for k in range(2):
                                mm = nc.tensor.matmul(bank[6][:, t * D:(t + 1) * D], U[:, k, t * L:(t + 1) * L], u2[:, k, :],
                                                      start=(k == 0), stop=(k == 1))
                        mm.then_inc(s.o_ps, 1)

                run(pe, NQ + 4, 2, 6, 4, update_step)


_INS = ["x", "src", "dst", "edge_attr_128", "L0_gnn_re_w1", "L0_gnn_re_b1", "L0_gnn_re_w2", "L0_gnn_re_b2",
        "L0_gnn_ea_w1", "L0_gnn_ea_b1", "L0_gnn_ea_w2", "L0_gnn_ea_b2"]


def kernel(**inputs):
    import numpy as _np
    import concourse.bacc as _bacc
    from concourse import mybir as _mybir
    from concourse.bass_utils import run_bass_kernel_spmd as _run

    nc = _bacc.Bacc("TRN2", target_bir_lowering=False, num_devices=1)
    arrays, args = {}, []
    for name in _INS:
        a = _np.ascontiguousarray(inputs[name])
        arrays[f"in_{name}"] = a
        args.append(nc.dram_tensor(f"in_{name}", a.shape, _mybir.dt.from_np(a.dtype), kind="ExternalInput").ap())
    shape = arrays["in_x"].shape
    args.append(nc.dram_tensor("out_x", shape, _mybir.dt.float32, kind="ExternalOutput").ap())
    bass_gnn_preln_layer_kernel(nc, *args)
    r = _run(nc, [arrays], core_ids=[0])
    return r.results[0]["out_x"]
```

```python
import concourse.bass as bass
from concourse import mybir
from contextlib import ExitStack


def bass_gnn_preln_layer_kernel(nc, x, src, dst, edge_attr, re_w1, re_b1, re_w2, re_b2,
                                ea_w1, ea_b1, ea_w2, ea_b2, out):
    f32, f32r = mybir.dt.float32, mybir.dt.float32r
    bf16, i32 = mybir.dt.bfloat16, mybir.dt.int32
    ALU = mybir.AluOpType
    ACT = mybir.ActivationFunctionType
    AX = mybir.AxisListType.X

    L = 128
    N, D = x.shape
    E = src.shape[0]
    HID = re_w1.shape[1]
    EPS = 1e-5

    QUAD = 4
    NQ = -(-N // (QUAD * L))
    NT = NQ * QUAD
    NPAD = NT * L
    FULL = N // L
    REST = N - FULL * L
    NTR = -(-N // L)
    XQ = [0, 2, 5, *range(10, NQ, 5), NQ]
    NXC = len(XQ) - 1

    TG = 14
    GE = TG * L
    NG = -(-E // GE)
    TAIL0 = E - GE
    OVER = NG * GE - E
    WIN = L
    PAIRS = TG // 2
    NU = NG * PAIRS
    AW = HID + 2
    DUMMY = NPAD
    NE = -(-E // L)
    GTAIL0 = E - L
    GOVER = NE * L - E
    OUTSIDE = -1000.0
    UNROLL = 2 * PAIRS

    LAG = 15
    AHEAD = 2
    NSTEP = NTR + LAG + 2
    NZ = max(NT + 1, NG + 4)

    P_dram = nc.dram_tensor("P_dram", [NPAD, HID], f32).ap()
    Q_dram = nc.dram_tensor("Q_dram", [NPAD, HID], f32).ap()
    sums_dram = nc.dram_tensor("sums_dram", [NZ * L, AW], f32).ap()
    local_dram = nc.dram_tensor("local_dram", [NG, GE], f32).ap()
    local_row_dram = nc.dram_tensor("local_row_dram", [NG, GE], bf16).ap()

    ctx = ExitStack()
    with ctx:
        def sb(name, shape, dt=f32):
            return ctx.enter_context(nc.sbuf_tensor(name, shape, dt))

        def sem(name):
            return ctx.enter_context(nc.semaphore(name))

        bank = [ctx.enter_context(nc.psum_tensor(f"bank{i}", [L, 512], f32)) for i in range(8)]

        w1a = sb("w1a", [L, HID])
        w1b = sb("w1b", [L, HID])
        w1c = sb("w1c", [L, HID])
        whi = sb("whi", [L, HID], f32r)
        wlo = sb("wlo", [L, HID], f32r)
        b1_all = sb("b1_all", [L, HID])
        w2 = sb("w2", [L, 2, D])
        b2_all = sb("b2_all", [L, D])
        u1 = sb("u1", [L, 2, HID])
        c1 = sb("c1", [L, 2])
        u2 = sb("u2", [L, 2, D])
        c2_all = sb("c2_all", [L, D])
        ident = sb("ident", [L, L])
        iota_free = sb("iota_free", [L, L])
        minus_part = sb("minus_part", [L, 1])
        pace = sb("pace", [L, 1])
        eps_col = sb("eps_col", [L, 1])
        one_col = sb("one_col", [L, 1])
        ones = sb("ones", [L, L])
        zeros = sb("zeros", [L, AW])
        flag = sb("flag", [L, 1], i32)

        x_all = sb("x_all", [L, NT, D])
        hT_all = sb("hT_all", [L, NPAD])

        AREA = 37 * 1024
        area = sb("area", [L, AREA // 4])

        class Lay:
            def __init__(self):
                self.at = 0

            def __call__(self, *shape, dt=f32):
                n = 1
                for extent in shape:
                    n *= extent
                words = -(-n * {f32: 4, i32: 4, bf16: 2}[dt] // 4)
                a = area[:, self.at:self.at + words]
                self.at += words
                assert self.at * 4 <= AREA
                if dt != f32:
                    a = a.bitcast(dt)
                if len(shape) == 2:
                    a = a.rearrange("p (a b) -> p a b", a=shape[0])
                if len(shape) == 3:
                    a = a.rearrange("p (a b c) -> p a b c", a=shape[0], b=shape[1])
                return a

        early = Lay()
        recv = early(GE, dt=i32)
        local = early(GE)
        local_row = early(GE, dt=bf16)
        first = early(1)
        lead = early(1)
        most = early(1)
        least = early(1)
        outside = early(4)
        faults = early(1)
        stats = early(2, QUAD * 6)
        mv = early(2, QUAD * 2)
        std = early(2, QUAD)
        rstd = early(2, QUAD)
        shift = early(2, QUAD)
        h_quad = early(2, QUAD, D)
        hT = early(2, QUAD * L)
        P_out = early(2, QUAD, HID)

        late = Lay()
        P_in = late(2, TG, HID)
        pre = late(2, 2, HID)

        e_in = sb("e_in", [L, 2, TG, D])
        row = sb("row", [L, 2, GE], bf16)
        col = sb("col", [L, 2, TG])
        idx = sb("idx", [L, 4, TG], i32)
        hTw = sb("hTw", [L, 2, L])
        Qhi = sb("Qhi", [L, 2, HID], f32r)
        Qlo = sb("Qlo", [L, 2, HID], f32r)
        ehi = sb("ehi", [L, 2, 2 * L], f32r)
        elo = sb("elo", [L, 2, 2 * L], f32r)
        dist = sb("dist", [L, 2, 2 * L])
        ohT = sb("ohT", [L, 2, 2, L], f32r)
        oh = sb("oh", [L, 2, 2, L], f32r)
        hhi = sb("hhi", [L, 2, 2, AW], f32r)
        hlo = sb("hlo", [L, 2, 2, AW], f32r)
        win = sb("win", [L, AW])
        win_out = sb("win_out", [L, 2, AW])

        gen = Lay()
        g_src = gen(1, dt=i32)
        g_dst = gen(1, dt=i32)
        g_dst_row = gen(L, dt=i32)
        g_e = gen(D)
        g_P = gen(HID)
        g_Q = gen(HID)
        g_eT = gen(L)
        g_recv = gen(1)
        g_recv_row = gen(L)
        g_same = gen(L)
        g_earlier = gen(L)
        g_count = gen(1)
        g_again = gen(1)
        g_away = gen(1)
        g_row = gen(1, dt=i32)
        g_hidden = gen(HID)
        g_h = gen(AW)
        g_sum = gen(AW)
        below = gen(L)
        all_edges = gen(1)
        new_edges = gen(1)
        dummy_row = gen(1)
        g_hT = gen(QUAD * L)
        g_Q_out = gen(QUAD, HID)

        S_in = sb("S_in", [L, 2, AW])
        ST = sb("ST", [L, 2 * L])
        eff = sb("eff", [L, D])
        effT = sb("effT", [L, L])
        U = sb("U", [L, 2, L])
        xc = sb("xc", [L, D])
        o_out = sb("o_out", [L, 2, D])

        names = """w1a_in b1_in weights_in ident0 consts zeroed dst_in first_ok lead_ok local_ok range_ok outside_ok
            faults_ok flag_ps flag_ok tail_masked row_ok local_st x_pad x_rest_in whi_ok wlo_ok fills
            stat_ok agg_ok std_ok rstd_ok shift_ok h_ok hT_ps hT_ok hT_kept P_ps P_ok P_st0 P_st1
            e_in0 e_in1 col_in0 col_in1 row_in0 row_in1 idx_in0 idx_in1 idx_in2 idx_in3 hTw_in0 hTw_in1
            zero_st0 zero_st1 zero_st2 zero_st3
            Qw_ps Qhi_ok Qlo_ok eT_ps ehi_ok elo_ok dist_ok ohT_ok pre_ps pre_ok hi_ok lo_ok oh_ok sums_ps
            win_in win_ok win_st
            S_in0 S_in1 ST_ps ST_ok eff_ps eff_ok effT_ps effT_ok U_ps U_ok xc_ok o_ps o_ok o_st0 o_st1
            g_free g_zero_st g_hT_ok g_Q_ps g_Q_ok g_Q_st g_ready g_in g_pool g_masks g_rows g_chain g_eT_ps g_eT_ok
            g_pre_ps g_h_ok g_sum_ps g_sum_ok g_scattered""".split()
        s = type("Sems", (), {n: sem(n) for n in names})
        passed = {e: sem(f"passed_{n}") for n, e in (("pool", nc.gpsimd.engine), ("sp", nc.sync.engine), ("dve", nc.vector.engine))}
        gathered = [[sem(f"gathered{b}_{u}") for u in range(PAIRS)] for b in range(2)]
        x_in = [sem(f"x_in{c}") for c in range(NXC)]
        P_st = [s.P_st0, s.P_st1]
        e_sem, col_sem, row_sem = [s.e_in0, s.e_in1], [s.col_in0, s.col_in1], [s.row_in0, s.row_in1]
        hTw_sem, idx_sem = [s.hTw_in0, s.hTw_in1], [s.idx_in0, s.idx_in1, s.idx_in2, s.idx_in3]
        zero_sem = [s.zero_st0, s.zero_st1, s.zero_st2, s.zero_st3]
        S_sem, o_st = [s.S_in0, s.S_in1], [s.o_st0, s.o_st1]

        hT_bank, P_bank = [bank[0], bank[3]], [bank[1:3], bank[4:6]]
        eT_bank, pre_bank, sums_bank = bank[0:2], bank[2:4], bank[4:6]
        node_bank = bank[6:8]

        P_rows = P_dram.rearrange("(q t p) c -> q p t c", t=QUAD, p=L)
        Q_rows = Q_dram.rearrange("(q t p) c -> q p t c", t=QUAD, p=L)
        x_rows = x[0:FULL * L, :].rearrange("(t p) d -> p t d", p=L)

        class Step:

            def __init__(self, k, turn=None, unroll=0, loops=1):
                self.k, self.turn, self.unroll, self.loops = k, turn, unroll, loops
                self.i = k if turn is None else turn * unroll + k
                self.last = k + (loops - 1) * unroll

            def back(self, n):
                return Step(self.k - n, self.turn, self.unroll, self.loops)

            def group(self, size, shift=0):
                return Step((self.k + shift) // size, self.turn, self.unroll // size, self.loops)

            def uses(self, buffers):
                return self.group(buffers).i + 1

            def within(self, n):
                inside = 0 <= self.k and self.last < n
                assert inside or self.last < 0 or self.k >= n, (self.k, self.last, n)
                return inside

            def least(self, n):
                assert self.k >= n or self.last < n, (self.k, self.last, n)
                return self.k >= n

            def span(self, size):
                return bass.ds(self.i * size, size)

        def run(eng, n, step, unroll=1, loops=()):
            k = 0
            for a, b in (*loops, (n, n)):
                while k < a:
                    step(Step(k))
                    k += 1
                if b > a:
                    assert (b - a) % unroll == 0 and b <= n
                    with eng.Fori(0, (b - a) // unroll) as turn:
                        for at in range(unroll):
                            step(Step(a + at, turn, unroll, (b - a) // unroll))
                    k = b

        def rounded(a, b, unroll):
            return (a, a + max(0, b - a) // unroll * unroll)

        GROUP_LOOPS = [rounded(4, LAG + 2, 4), rounded(LAG + 5, NG - 1, 4)]
        EDGE_LOOPS = [rounded(4 * PAIRS, (LAG + 2) * PAIRS, UNROLL), rounded((LAG + 5) * PAIRS, (NG - 1) * PAIRS, UNROLL)]

        def apart(eng):
            eng.sem_inc(passed[eng.engine], 1)

        def either(eng, windowed, general):
            eng.wait_ge(s.flag_ok, 1)
            outsiders = eng.value_load(flag[0:1, 0:1], min_val=0, max_val=4 * NG)
            with eng.If(outsiders > 0):
                general()
            with eng.Else():
                windowed()

        with nc.Block() as block:

            @block.sync
            def _(sp):
                def load_x(c):
                    t0, t1 = XQ[c] * QUAD, min(XQ[c + 1] * QUAD, FULL)
                    sp.dma_start(x_all[:, t0:t1, :], x_rows[:, t0:t1, :]).then_inc(x_in[c], 16)

                load_x(0)
                sp.dma_start(recv[0:NG - 1, :], dst[0:(NG - 1) * GE].rearrange("(g e) -> g e", e=GE)).then_inc(s.dst_in, 16)
                sp.dma_start(recv[NG - 1:NG, :], dst[TAIL0:E].rearrange("(g e) -> g e", e=GE)).then_inc(s.dst_in, 16)
                for c in range(1, NXC):
                    load_x(c)
                sp.wait_ge(s.x_pad, 1)
                sp.dma_start(x_all[0:REST, FULL, :], x[FULL * L:N, :]).then_inc(s.x_rest_in, 16)

                def store_P(q):
                    sp.wait_ge(s.P_ok, 2 * (q.i + 1))
                    if q.turn is not None:
                        apart(sp)
                    sp.dma_start(P_rows[bass.ds(q.i, 1)].rearrange("o p t c -> (o p) t c"),
                                 P_out[:, q.k % 2, :, :]).then_inc(P_st[q.k % 2], 16)
                    if q.turn is None and q.k == NQ - 2:
                        sp.wait_ge(s.tail_masked, 1)
                        sp.dma_start(local_dram, local[0:NG, :]).then_inc(s.local_st, 16)
                        sp.wait_ge(s.row_ok, 1)
                        sp.dma_start(local_row_dram, local_row[0:NG, :]).then_inc(s.local_st, 16)

                run(sp, NQ, store_P, 2, [rounded(2, NQ - 2, 2)])

                def edge_slice(g, size):
                    if g.turn is None:
                        e0 = TAIL0 if g.k == NG - 1 else g.k * GE
                        return slice(e0, e0 + size)
                    assert g.last < NG - 1
                    return bass.ds(g.i * GE, size)

                def window(g):
                    return sp.value_load(dst[edge_slice(g, 1)].rearrange("(o n) -> o n", o=1), min_val=0, max_val=N - 1)

                def load_idx(g):
                    if g.least(4):
                        sp.wait_ge(s.pre_ok, PAIRS * (g.i - 3))
                        apart(sp)
                    sp.dma_start(idx[:, g.k % 4, :], src[edge_slice(g, GE)].rearrange("(p t) -> p t", t=TG)).then_inc(idx_sem[g.k % 4], 16)

                def load_group(g):
                    b = g.k % 2
                    node = window(g)
                    if g.least(2):
                        sp.wait_ge(s.dist_ok, PAIRS * (g.i - 1))
                        sp.wait_ge(s.oh_ok, PAIRS * (g.i - 1))
                        sp.wait_ge(s.Qw_ps, g.i - 1)
                        sp.wait_ge(s.eT_ps, PAIRS * (g.i - 1))
                        apart(sp)
                    sp.dma_start(row[:, b, :], local_row_dram[bass.ds(g.i, 1), :].rearrange("o e -> (o e)").partition_broadcast(L)).then_inc(row_sem[b], 16)
                    sp.dma_start(e_in[:, b, :, :], edge_attr[edge_slice(g, GE), :].rearrange("(p t) d -> p t d", t=TG)).then_inc(e_sem[b], 16)
                    sp.dma_start(hTw[:, b, :], hT_all[:, bass.ds(node, WIN)]).then_inc(hTw_sem[b], 16)
                    sp.dma_start(col[:, b, :], local_dram[bass.ds(g.i, 1), :].rearrange("o (p t) -> (o p) t", t=TG)).then_inc(col_sem[b], 16)

                def zero_tile(t):
                    sp.dma_start(sums_dram[t.span(L), :], zeros[:, :]).then_inc(zero_sem[t.k % 4], 16)

                def load_window(g, tiles):
                    node = window(g)
                    if g.least(1):
                        sp.wait_ge(s.win_st, 16 * g.i)
                    for t in tiles:
                        if t.within(NZ):
                            sp.wait_ge(zero_sem[t.k % 4], 16 * t.uses(4))
                    if g.turn is not None:
                        apart(sp)
                    sp.dma_start(win[:, :], sums_dram[bass.ds(node, WIN), :]).then_inc(s.win_in, 16)

                def load_sums(t):
                    if t.least(2):
                        sp.wait_ge(s.eff_ok, t.i - 1)
                        apart(sp)
                    sp.dma_start(S_in[:, t.k % 2, :], sums_dram[t.span(L), :]).then_inc(S_sem[t.k % 2], 16)

                def store_out(t):
                    sp.wait_ge(s.o_ok, t.i + 1)
                    if t.turn is None and t.k == FULL:
                        sp.dma_start(out[FULL * L:N, :], o_out[0:REST, t.k % 2, :]).then_inc(o_st[t.k % 2], 16)
                    else:
                        assert t.last < FULL
                        apart(sp)
                        sp.dma_start(out[t.span(L), :], o_out[:, t.k % 2, :]).then_inc(o_st[t.k % 2], 16)

                def group_step(g):
                    if g.back(-1).within(NG):
                        load_idx(g.back(-1))
                    if g.within(NG):
                        load_group(g)
                    if g.back(-4).within(NZ):
                        zero_tile(g.back(-4))
                    stored = g.back(2)
                    if stored.within(NG):
                        node = window(stored)
                        sp.wait_ge(s.win_ok, stored.i + 1)
                        apart(sp)
                        sp.dma_start(sums_dram[bass.ds(node, WIN), :], win_out[:, stored.k % 2, :]).then_inc(s.win_st, 16)
                        if g.back(1).within(NG):
                            load_window(g.back(1), [g.back(-1)])
                        elif stored.k == NG - 1:
                            sp.wait_ge(s.win_st, 16 * NG)
                    t = g.back(LAG + 2)
                    if t.within(NTR):
                        load_sums(t)
                    if t.back(1).within(NTR):
                        store_out(t.back(1))

                def windowed():
                    sp.wait_ge(s.local_st, 32)
                    sp.wait_ge(s.hT_kept, NQ)
                    load_idx(Step(0))
                    sp.wait_ge(s.zeroed, 1)
                    for t in range(4):
                        zero_tile(Step(t))
                    run(sp, 2, lambda g: (load_window(Step(0), [Step(t) for t in range(3)]) if g.k == 1 else None, group_step(g)))
                    loops = [(a - 2, b - 2) for a, b in GROUP_LOOPS]
                    run(sp, NSTEP + 1 - 2, lambda g: group_step(g.back(-2)), 4, loops)

                def general():
                    for b in range(2):
                        sp.wait_ge(P_st[b], 16 * ((NQ + 1 - b) // 2))
                    sp.wait_ge(s.local_st, 32)
                    sp.wait_ge(s.zeroed, 1)
                    sp.sem_inc(s.g_free, 1)
                    run(sp, NZ, lambda t: sp.dma_start(sums_dram[t.span(L), :], zeros[:, :]).then_inc(s.g_zero_st, 16), 1, [(0, NZ)])

                    def store_Q(q):
                        sp.wait_ge(s.g_Q_ok, 2 * (q.i + 1))
                        apart(sp)
                        sp.dma_start(Q_rows[bass.ds(q.i, 1)].rearrange("o p t c -> (o p) t c"), g_Q_out[:, :, :]).then_inc(s.g_Q_st, 16)

                    run(sp, NQ, store_Q, 1, [(0, NQ)])
                    sp.wait_ge(s.g_zero_st, 16 * NZ)
                    sp.wait_ge(s.g_Q_st, 16 * NQ)
                    sp.sem_inc(s.g_ready, 1)

                    def tile_step(i):
                        if i.least(1):
                            sp.wait_ge(s.g_scattered, 16 * i.i)
                            apart(sp)
                        e = bass.ds(GTAIL0, L) if i.turn is None and i.k == NE - 1 else i.span(L)
                        sp.dma_start(g_src[:, :], src[e].rearrange("(p o) -> p o", o=1)).then_inc(s.g_in, 16)
                        sp.dma_start(g_dst[:, :], dst[e].rearrange("(p o) -> p o", o=1)).then_inc(s.g_in, 16)
                        sp.dma_start(g_dst_row[:, :], dst[e].partition_broadcast(L)).then_inc(s.g_in, 16)
                        sp.dma_start(g_e[:, :], edge_attr[e, :]).then_inc(s.g_in, 16)

                    run(sp, NE, tile_step, 1, [(1, NE - 1)])
                    sp.wait_ge(s.g_scattered, 16 * NE)

                    def node_tile(t):
                        if t.within(NTR):
                            load_sums(t)
                        if t.back(1).within(NTR):
                            store_out(t.back(1))

                    run(sp, NTR + 1, node_tile, 2, [rounded(4, NTR - 1, 2)])

                either(sp, windowed, general)
                for b in range(2):
                    sp.wait_ge(o_st[b], 16 * ((NTR + 1 - b) // 2))

            @block.gpsimd
            def _(pool):
                nc.gpsimd.memset(x_all[:, FULL:NT, :], 0.0).then_inc(s.x_pad, 1)
                nc.gpsimd.memset(ident[:], 0.0).then_inc(s.ident0, 1)
                nc.gpsimd.memset(eps_col[:], EPS).then_inc(s.consts, 1)
                nc.gpsimd.memset(one_col[:], 1.0).then_inc(s.consts, 1)
                nc.gpsimd.memset(ones[:], 1.0).then_inc(s.consts, 1)
                pool.wait_ge(s.ident0, 1)
                nc.gpsimd.affine_select(out=ident[:], in_=ident[:], compare_op=ALU.not_equal, fill=1.0, base=0,
                                        pattern=[[-1, L]], channel_multiplier=1).then_inc(s.consts, 1)
                nc.gpsimd.iota(iota_free[:], pattern=[[1, L]], base=0, channel_multiplier=0,
                               allow_small_or_imprecise_dtypes=True).then_inc(s.consts, 1)
                nc.gpsimd.iota(minus_part[:], pattern=[[0, 1]], base=0, channel_multiplier=-1,
                               allow_small_or_imprecise_dtypes=True).then_inc(s.consts, 1)
                nc.gpsimd.iota(pace[:], pattern=[[0, 1]], base=0, channel_multiplier=L,
                               allow_small_or_imprecise_dtypes=True).then_inc(s.consts, 1)
                nc.gpsimd.memset(zeros[:], 0.0).then_inc(s.zeroed, 1)

                def keep(q):
                    if q.turn is None and q.k == 4:
                        pool.wait_ge(s.range_ok, 2)
                        pool.wait_ge(s.consts, 7)
                        pool.wait_ge(s.zeroed, 1)
                        pool.wait_ge(s.hT_kept, 4)
                        q0 = (NG - 1) // 32 * 32
                        nc.gpsimd.affine_select(out=local[q0:NG, 0:OVER], in_=local[q0:NG, 0:OVER], compare_op=ALU.not_equal,
                                                fill=OUTSIDE, base=q0 - (NG - 1), pattern=[[0, OVER]],
                                                channel_multiplier=1).then_inc(s.tail_masked, 1)
                        pool.wait_ge(s.tail_masked, 1)
                    pool.wait_ge(s.hT_ok, q.i + 1)
                    nc.gpsimd.tensor_copy(hT_all[:, q.span(QUAD * L)], hT[:, q.k % 2, :]).then_inc(s.hT_kept, 1)

                run(pool, NQ, keep, 2, [rounded(5, NQ, 2)])

                def windowed():
                    for b in range(2):
                        pool.wait_ge(P_st[b], 16 * ((NQ + 1 - b) // 2))
                    pool.wait_ge(s.local_st, 32)

                    def gather(g):
                        b = g.k % 2
                        pool.wait_ge(idx_sem[g.k % 4], 16 * g.uses(4))
                        apart(pool)
                        for u in range(PAIRS):
                            if g.least(2):
                                pool.wait_ge(s.pre_ok, PAIRS * (g.i - 2) + u + 1)
                                apart(pool)
                            for t in (2 * u, 2 * u + 1):
                                nc.gpsimd.indirect_dma_start(
                                    out=P_in[:, b, t, :], out_offset=None, in_=P_dram[:, :],
                                    in_offset=bass.IndirectOffsetOnAxis(ap=idx[:, g.k % 4, t:t + 1], axis=0)
                                ).then_inc(gathered[b][u], 16)

                    run(pool, NG, gather, 4, [rounded(4, NG, 4)])

                def general():
                    pool.wait_ge(s.g_free, 1)
                    nc.gpsimd.memset(below[:], 1.0).then_inc(s.g_pool, 1)
                    nc.gpsimd.memset(all_edges[:], 1.0).then_inc(s.g_masks, 1)
                    nc.gpsimd.memset(new_edges[:], 1.0).then_inc(s.g_pool, 1)
                    nc.gpsimd.iota(dummy_row[:], pattern=[[0, 1]], base=DUMMY, channel_multiplier=1,
                                   allow_small_or_imprecise_dtypes=True).then_inc(s.g_masks, 1)
                    pool.wait_ge(s.g_pool, 2)
                    nc.gpsimd.affine_select(out=below[:], in_=below[:], compare_op=ALU.is_ge, fill=0.0, base=-1,
                                            pattern=[[-1, L]], channel_multiplier=1).then_inc(s.g_masks, 1)
                    nc.gpsimd.affine_select(out=new_edges[:], in_=new_edges[:], compare_op=ALU.is_ge, fill=0.0, base=-GOVER,
                                            pattern=[[0, 1]], channel_multiplier=1).then_inc(s.g_masks, 1)
                    pool.wait_ge(s.g_ready, 1)

                    def tile_step(i):
                        pool.wait_ge(s.g_in, 64 * (i.i + 1))
                        apart(pool)
                        for rows, table, index in ((g_P, P_dram, g_src), (g_Q, Q_dram, g_dst)):
                            nc.gpsimd.indirect_dma_start(
                                out=rows[:, :], out_offset=None, in_=table[:, :],
                                in_offset=bass.IndirectOffsetOnAxis(ap=index[:, 0:1], axis=0)).then_inc(s.g_rows, 16)
                        pool.wait_ge(s.g_sum_ok, i.i + 1)
                        apart(pool)
                        nc.gpsimd.indirect_dma_start(
                            out=sums_dram[:, :], out_offset=bass.IndirectOffsetOnAxis(ap=g_row[:, 0:1], axis=0),
                            in_=g_sum[:, :], in_offset=None, compute_op=ALU.add).then_inc(s.g_scattered, 16)

                    run(pool, NE, tile_step, 1, [(0, NE)])

                either(pool, windowed, general)

            @block.scalar
            def _(act):
                act.dma_start(w1a[:, :], re_w1[0:D, :]).then_inc(s.w1a_in, 16)
                act.dma_start(b1_all[:, :], re_b1.partition_broadcast(L)).then_inc(s.b1_in, 16)
                for tile, source in ((w1b[:, :], re_w1[D:2 * D, :]), (w1c[:, :], re_w1[2 * D:3 * D, :]),
                                     (w2[:, :, :], re_w2.rearrange("(k p) n -> p k n", p=L)),
                                     (b2_all[:, :], re_b2.partition_broadcast(L)),
                                     (u1[:, :, :], ea_w1.rearrange("(k p) n -> p k n", p=L)),
                                     (u2[:, :, :], ea_w2.rearrange("(k p) n -> p k n", p=L)),
                                     (c2_all[:, :], ea_b2.partition_broadcast(L))):
                    act.dma_start(tile, source).then_inc(s.weights_in, 16)
                with nc.allow_non_contiguous_dma(reason="256 biases, two to a partition"):
                    act.dma_start(c1[:, :], ea_b1.rearrange("(k p) -> p k", p=L)).then_inc(s.weights_in, 16)
                act.wait_ge(s.consts, 7)

                def take_std(q):
                    act.wait_ge(s.agg_ok, QUAD * (q.i + 1))
                    if q.least(2):
                        act.wait_ge(s.rstd_ok, q.i - 1)
                    b = q.k % 2
                    nc.scalar.activation(std[:, b, :], mv[:, b, :].rearrange("p (t c) -> p t c", c=2)[:, :, 1],
                                         ACT.Sqrt, bias=eps_col[:, 0:1]).then_inc(s.std_ok, 1)

                def normalise(q):
                    act.wait_ge(s.shift_ok, q.i + 1)
                    if q.least(2):
                        act.wait_ge(s.hT_ps, q.i - 1)
                    for t in range(QUAD):
                        h = nc.scalar.activation(h_quad[:, q.k % 2, t, :], x_all[:, bass.ds(q.i * QUAD + t, 1), :].rearrange("p o d -> p (o d)"),
                                                 ACT.Relu, bias=shift[:, q.k % 2, t:t + 1], scale=rstd[:, q.k % 2, t:t + 1])
                    h.then_inc(s.h_ok, 1)

                take_std(Step(0))
                normalise(Step(0))
                take_std(Step(1))

                def node_step(q):
                    if q.back(-1).within(NQ):
                        normalise(q.back(-1))
                    act.wait_ge(s.hT_ps, q.i + 1)
                    if q.least(2):
                        act.wait_ge(s.P_ps, 2 * (q.i - 1))
                        act.wait_ge(s.hT_kept, q.i - 1)
                    nc.scalar.copy(hT[:, q.k % 2, :], hT_bank[q.k % 2][:, :]).then_inc(s.hT_ok, 1)
                    if q.back(-2).within(NQ):
                        take_std(q.back(-2))

                run(act, NQ, node_step, 2, [rounded(2, NQ - 2, 2)])

                act.wait_ge(s.weights_in, 128)
                nc.scalar.copy(whi[:, :], w1c[:, :]).then_inc(s.whi_ok, 1)

                def q_hi(g):
                    act.wait_ge(s.Qw_ps, g.i + 1)
                    if g.least(2):
                        act.wait_ge(s.pre_ps, PAIRS * (g.i - 1))
                    nc.scalar.copy(Qhi[:, g.k % 2, :], node_bank[1][:, 0:HID]).then_inc(s.Qhi_ok, 1)

                def take_distance(u):
                    g, at = u.group(PAIRS), u.k % PAIRS
                    if at == 0:
                        act.wait_ge(row_sem[g.k % 2], 16 * g.uses(2))
                    if u.least(2):
                        act.wait_ge(s.ohT_ok, u.i - 1)
                    nc.scalar.activation(dist[:, u.k % 2, :], row[:, g.k % 2, 2 * L * at:2 * L * (at + 1)],
                                         ACT.Abs, bias=minus_part[:, 0:1]).then_inc(s.dist_ok, 1)

                def node_slot(at, t):
                    if at == 0:
                        act.wait_ge(s.ST_ps, t.i + 1)
                        if t.least(1):
                            act.wait_ge(s.eff_ps, t.i)
                        nc.scalar.copy(ST[:, :], node_bank[0][:, 0:2 * L]).then_inc(s.ST_ok, 1)
                    if at == 2:
                        act.wait_ge(s.effT_ps, t.i + 1)
                        if t.least(1):
                            act.wait_ge(s.U_ps, t.i)
                        nc.scalar.copy(effT[:, :], node_bank[0][:, 0:L]).then_inc(s.effT_ok, 1)
                    if at == 3:
                        act.wait_ge(s.U_ps, t.i + 1)
                        if t.least(1):
                            act.wait_ge(s.o_ps, t.i)
                        for k in range(2):
                            nc.scalar.activation(U[:, k, :], node_bank[1][:, k * L:(k + 1) * L], ACT.Relu,
                                                 bias=c1[:, k:k + 1]).then_inc(s.U_ok, 1)

                def edge_step(u):
                    if u.within(NU):
                        act.wait_ge(s.eT_ps, u.i + 1)
                        if u.least(2):
                            act.wait_ge(s.pre_ps, u.i - 1)
                        nc.scalar.copy(ehi[:, u.k % 2, :], eT_bank[u.k % 2][:, 0:2 * L]).then_inc(s.ehi_ok, 1)
                    v = u.back(2)
                    if v.within(NU):
                        act.wait_ge(s.pre_ok, v.i + 1)
                        if v.least(2):
                            act.wait_ge(s.sums_ps, v.i - 1)
                        nc.scalar.activation(hhi[:, v.k % 2, :, 0:HID], pre[:, v.k % 2, :, :], ACT.Relu).then_inc(s.hi_ok, 1)
                    if u.within(NU):
                        act.wait_ge(s.dist_ok, u.i + 1)
                        nc.scalar.activation(ohT[:, u.k % 2, :, :].rearrange("p t e -> p (t e)"), dist[:, u.k % 2, :],
                                             ACT.Relu, bias=one_col[:, 0:1], scale=-1.0).then_inc(s.ohT_ok, 1)
                    if u.back(-1).within(NU):
                        take_distance(u.back(-1))
                    g, at = u.group(PAIRS), u.k % PAIRS
                    if g.back(LAG + 2).within(NTR):
                        node_slot(at, g.back(LAG + 2))
                    if at == 5 and g.back(-1).within(NG):
                        q_hi(g.back(-1))

                def windowed():
                    act.wait_ge(s.local_st, 32)
                    take_distance(Step(0))
                    q_hi(Step(0))
                    run(act, NSTEP * PAIRS, edge_step, UNROLL, EDGE_LOOPS)

                def general():
                    act.wait_ge(s.g_free, 1)
                    act.wait_ge(s.hT_kept, NQ)

                    def hT_step(q):
                        if q.least(1):
                            act.wait_ge(s.g_Q_ps, 2 * q.i)
                        nc.scalar.copy(g_hT[:, :], hT_all[:, q.span(QUAD * L)]).then_inc(s.g_hT_ok, 1)

                    run(act, NQ, hT_step, 1, [(1, NQ)])

                    def tile_step(i):
                        act.wait_ge(s.g_eT_ps, i.i + 1)
                        nc.scalar.copy(g_eT[:, :], eT_bank[0][:, 0:L]).then_inc(s.g_eT_ok, 1)

                    run(act, NE, tile_step, 1, [(0, NE)])
                    run(act, NTR, lambda t: [node_slot(at, t) for at in (0, 2, 3)], 1, [(2, NTR)])

                either(act, windowed, general)

            @block.vector
            def _(dve):
                nc.vector.memset(outside[:], 0.0).then_inc(s.first_ok, 1)
                nc.vector.memset(hhi[:, :, :, HID:AW].bitcast(f32), 1.0).then_inc(s.fills, 1)
                nc.vector.memset(hlo[:, :, :, HID:AW].bitcast(f32), 0.0).then_inc(s.fills, 1)

                def count_locals():
                    dve.wait_ge(s.dst_in, 32)
                    nc.vector.tensor_copy(first[0:NG, :], recv[0:NG, 0:1]).then_inc(s.first_ok, 1)
                    dve.wait_ge(s.first_ok, 2)
                    nc.vector.tensor_scalar(local[0:NG, :], recv[0:NG, :], first[0:NG, 0:1], None, ALU.subtract).then_inc(s.local_ok, 1)
                    dve.wait_ge(s.consts, 7)
                    nc.vector.tensor_tensor(lead[0:NG, :], first[0:NG, :], pace[0:NG, :], ALU.subtract).then_inc(s.lead_ok, 1)

                def take_range():
                    dve.wait_ge(s.local_ok, 1)
                    nc.vector.tensor_reduce(most[0:NG, :], local[0:NG, :], AX, ALU.max).then_inc(s.range_ok, 1)
                    nc.vector.tensor_reduce(least[0:NG, :], local[0:NG, :], AX, ALU.min).then_inc(s.range_ok, 1)

                def find_faults():
                    dve.wait_ge(s.range_ok, 2)
                    dve.wait_ge(s.lead_ok, 1)
                    nc.vector.tensor_scalar(outside[0:NG, 0:1], most[0:NG, :], float(WIN - 1), None, ALU.is_gt).then_inc(s.outside_ok, 1)
                    nc.vector.tensor_scalar(outside[0:NG, 1:2], least[0:NG, :], 0.0, None, ALU.is_lt).then_inc(s.outside_ok, 1)
                    nc.vector.tensor_scalar(outside[0:NG, 2:3], least[0:NG, :], lead[0:NG, 0:1], float(-LAG * L),
                                            ALU.add, ALU.is_lt).then_inc(s.outside_ok, 1)
                    nc.vector.tensor_scalar(outside[0:NG, 3:4], most[0:NG, :], lead[0:NG, 0:1], float(AHEAD * L - 1),
                                            ALU.add, ALU.is_gt).then_inc(s.outside_ok, 1)
                    dve.wait_ge(s.outside_ok, 4)
                    nc.vector.tensor_reduce(faults[:, :], outside[:, :], AX, ALU.add).then_inc(s.faults_ok, 1)

                def turn_rows():
                    dve.wait_ge(s.tail_masked, 1)
                    nc.vector.tensor_copy(local_row[0:NG, :].rearrange("g (t p) -> g p t", p=L),
                                          local[0:NG, :].rearrange("g (p t) -> g p t", t=TG)).then_inc(s.row_ok, 1)
                    dve.wait_ge(s.flag_ps, 1)
                    nc.vector.tensor_copy(flag[:, :], node_bank[1][:, 0:1]).then_inc(s.flag_ok, 1)

                def take_stats(q):
                    b = q.k % 2
                    if q.turn is None and q.k in XQ[:-1]:
                        dve.wait_ge(x_in[XQ.index(q.k)], 16)
                        if q.k == XQ[-2]:
                            dve.wait_ge(s.x_rest_in, 16)
                    if q.least(2):
                        dve.wait_ge(s.std_ok, q.i - 1)
                        dve.wait_ge(s.shift_ok, q.i - 1)
                    for t in range(QUAD):
                        nc.vector.bn_stats(stats[:, b, 6 * t:6 * t + 6],
                                           x_all[:, bass.ds(q.i * QUAD + t, 1), :].rearrange("p o d -> p (o d)")).then_inc(s.stat_ok, 1)
                    for t in range(QUAD):
                        dve.wait_ge(s.stat_ok, QUAD * q.i + t + 1)
                        if q.turn is not None:
                            apart(dve)
                        nc.vector.bn_aggr(mv[:, b, 2 * t:2 * t + 2], stats[:, b, 6 * t:6 * t + 6]).then_inc(s.agg_ok, 1)

                def take_rstd(q):
                    b = q.k % 2
                    dve.wait_ge(s.std_ok, q.i + 1)
                    if q.least(2):
                        dve.wait_ge(s.h_ok, q.i - 1)
                    nc.vector.reciprocal(rstd[:, b, :], std[:, b, :]).then_inc(s.rstd_ok, 1)
                    dve.wait_ge(s.rstd_ok, q.i + 1)
                    nc.vector.scalar_tensor_tensor(shift[:, b, :], mv[:, b, :].rearrange("p (t c) -> p t c", c=2)[:, :, 0],
                                                   -1.0, rstd[:, b, :], ALU.mult, ALU.mult).then_inc(s.shift_ok, 1)

                take_stats(Step(0))
                take_rstd(Step(0))
                take_stats(Step(1))
                dve.wait_ge(s.b1_in, 16)

                stage0 = {0: count_locals, 1: take_range, 3: find_faults, 8: turn_rows}

                def node_step(q):
                    if q.back(-1).within(NQ):
                        take_rstd(q.back(-1))
                    if q.back(-2).within(NQ):
                        take_stats(q.back(-2))
                    p = q.back(1)
                    if p.within(NQ):
                        if p.least(2):
                            dve.wait_ge(P_st[p.k % 2], 16 * (p.uses(2) - 1))
                        for half in range(2):
                            dve.wait_ge(s.P_ps, 2 * p.i + half + 1)
                            nc.vector.tensor_tensor(P_out[:, p.k % 2, 2 * half:2 * half + 2, :],
                                                    P_bank[p.k % 2][half][:, :].rearrange("p (t c) -> p t c", t=2),
                                                    b1_all[:, :].unsqueeze(1).to_broadcast([L, 2, HID]), ALU.add).then_inc(s.P_ok, 1)
                    if q.turn is None and q.k in stage0:
                        stage0[q.k]()

                run(dve, NQ + 1, node_step, 2, [rounded(a, b - 2, 2) for a, b in [(4, 10)] + [(a - 1, b) for a, b in zip(XQ[3:], XQ[4:])]])

                dve.wait_ge(s.weights_in, 128)
                dve.wait_ge(s.whi_ok, 1)
                nc.vector.tensor_tensor(wlo[:, :], w1c[:, :], whi[:, :].bitcast(f32), ALU.subtract).then_inc(s.wlo_ok, 1)

                def q_lo(g):
                    dve.wait_ge(s.Qhi_ok, g.i + 1)
                    if g.least(2):
                        dve.wait_ge(s.pre_ps, PAIRS * (g.i - 1))
                    nc.vector.tensor_tensor(Qlo[:, g.k % 2, :], node_bank[1][:, 0:HID], Qhi[:, g.k % 2, :].bitcast(f32), ALU.subtract).then_inc(s.Qlo_ok, 1)

                def node_slot(at, t):
                    if at == 2:
                        dve.wait_ge(s.eff_ps, t.i + 1)
                        if t.least(1):
                            dve.wait_ge(s.effT_ps, t.i)
                        nc.vector.scalar_tensor_tensor(eff[:, :], b2_all[:, :], S_in[:, t.k % 2, HID:HID + 1],
                                                       node_bank[1][:, 0:D], ALU.mult, ALU.add).then_inc(s.eff_ok, 1)
                    if at == 3:
                        if t.least(1):
                            dve.wait_ge(s.o_ok, t.i)
                        nc.vector.tensor_tensor(xc[:, :], x_all[:, bass.ds(t.i, 1), :].rearrange("p o d -> p (o d)"), c2_all[:, :],
                                                ALU.add).then_inc(s.xc_ok, 1)
                    if at == 5:
                        dve.wait_ge(s.o_ps, t.i + 1)
                        dve.wait_ge(s.xc_ok, t.i + 1)
                        if t.least(2):
                            dve.wait_ge(o_st[t.k % 2], 16 * (t.uses(2) - 1))
                        nc.vector.tensor_tensor(o_out[:, t.k % 2, :], node_bank[0][:, 0:D], xc[:, :], ALU.add).then_inc(s.o_ok, 1)

                def edge_step(u):
                    g, at = u.group(PAIRS), u.k % PAIRS
                    if g.back(LAG + 2).within(NTR):
                        node_slot(at, g.back(LAG + 2))
                    v = u.back(2)
                    if v.within(NU):
                        g, b, at = v.group(PAIRS), v.k % 2, v.k % PAIRS
                        dve.wait_ge(s.pre_ps, v.i + 1)
                        dve.wait_ge(gathered[g.k % 2][at], 32 * g.uses(2))
                        if v.least(2):
                            dve.wait_ge(s.lo_ok, v.i - 1)
                        nc.vector.tensor_tensor(pre[:, b, :, :], pre_bank[b][:, :].rearrange("p (t c) -> p t c", t=2),
                                                P_in[:, g.k % 2, 2 * at:2 * at + 2, :], ALU.add).then_inc(s.pre_ok, 1)
                    w = u.back(3)
                    if w.within(NU):
                        b = w.k % 2
                        dve.wait_ge(s.hi_ok, w.i + 1)
                        if w.least(2):
                            dve.wait_ge(s.sums_ps, w.i - 1)
                        nc.vector.scalar_tensor_tensor(hlo[:, b, :, 0:HID], pre[:, b, :, :], 0.0,
                                                       hhi[:, b, :, 0:HID].bitcast(f32), ALU.max, ALU.subtract).then_inc(s.lo_ok, 1)
                    if u.within(NU):
                        dve.wait_ge(s.ehi_ok, u.i + 1)
                        if u.least(2):
                            dve.wait_ge(s.pre_ps, u.i - 1)
                        nc.vector.tensor_tensor(elo[:, u.k % 2, :], eT_bank[u.k % 2][:, 0:2 * L], ehi[:, u.k % 2, :].bitcast(f32),
                                                ALU.subtract).then_inc(s.elo_ok, 1)
                    if v.within(NU):
                        g, at = v.group(PAIRS), v.k % PAIRS
                        if at == 0:
                            dve.wait_ge(col_sem[g.k % 2], 16 * g.uses(2))
                        if v.least(2):
                            dve.wait_ge(s.sums_ps, v.i - 1)
                        nc.vector.tensor_tensor(oh[:, v.k % 2, :, :], iota_free[:, :].unsqueeze(1).to_broadcast([L, 2, L]),
                                                col[:, g.k % 2, 2 * at:2 * at + 2].unsqueeze(2).to_broadcast([L, 2, L]),
                                                ALU.is_equal).then_inc(s.oh_ok, 1)
                    g, at = u.group(PAIRS), u.k % PAIRS
                    if at == 6 and g.back(-1).within(NG):
                        q_lo(g.back(-1))
                    if at == 3 and g.back(1).within(NG):
                        w = g.back(1)
                        dve.wait_ge(s.sums_ps, PAIRS * (w.i + 1))
                        dve.wait_ge(s.win_in, 16 * (w.i + 1))
                        if w.least(2):
                            dve.wait_ge(s.win_st, 16 * (w.i - 1))
                        nc.vector.tensor_tensor(win_out[:, w.k % 2, :], sums_bank[w.k % 2][:, 0:AW], win[:, :], ALU.add).then_inc(s.win_ok, 1)

                def windowed():
                    q_lo(Step(0))
                    run(dve, NSTEP * PAIRS, edge_step, UNROLL, EDGE_LOOPS)

                def general():
                    dve.wait_ge(s.g_free, 1)

                    def Q_step(q):
                        if q.least(1):
                            dve.wait_ge(s.g_Q_st, 16 * q.i)
                        for half in range(2):
                            dve.wait_ge(s.g_Q_ps, 2 * q.i + half + 1)
                            nc.vector.tensor_copy(g_Q_out[:, 2 * half:2 * half + 2, :],
                                                  P_bank[0][half][:, :].rearrange("p (t c) -> p t c", t=2)).then_inc(s.g_Q_ok, 1)

                    run(dve, NQ, Q_step, 1, [(1, NQ)])
                    dve.wait_ge(s.g_masks, 4)
                    LINKS = 11

                    def tile_step(i):
                        linked = [0]

                        def link(ins):
                            linked[0] += 1
                            ins.then_inc(s.g_chain, 1)
                            dve.wait_ge(s.g_chain, i.i * LINKS + linked[0])

                        dve.wait_ge(s.g_in, 64 * (i.i + 1))
                        link(nc.vector.tensor_copy(g_recv[:, :], g_dst[:, :]))
                        link(nc.vector.tensor_copy(g_recv_row[:, :], g_dst_row[:, :]))
                        link(nc.vector.tensor_scalar(g_same[:, :], g_recv_row[:, :], g_recv[:, 0:1], None, ALU.is_equal))
                        link(nc.vector.tensor_tensor(g_earlier[:, :], g_same[:, :], below[:, :], ALU.mult))
                        link(nc.vector.tensor_reduce(g_count[:, :], g_earlier[:, :], AX, ALU.add))
                        link(nc.vector.tensor_scalar(g_again[:, :], g_count[:, :], 1.0, None, ALU.min))
                        link(nc.vector.tensor_tensor(g_away[:, :], dummy_row[:, :], g_recv[:, :], ALU.subtract))
                        link(nc.vector.scalar_tensor_tensor(g_row[:, :], g_away[:, :], g_again[:, 0:1], g_recv[:, :],
                                                            ALU.mult, ALU.add))
                        real = new_edges if i.turn is None and i.k == NE - 1 else all_edges
                        dve.wait_ge(s.g_pre_ps, i.i + 1)
                        dve.wait_ge(s.g_rows, 32 * (i.i + 1))
                        link(nc.vector.tensor_tensor(g_hidden[:, :], P_bank[0][0][:, 0:HID], g_P[:, :], ALU.add))
                        link(nc.vector.tensor_tensor(g_hidden[:, :], g_hidden[:, :], g_Q[:, :], ALU.add))
                        link(nc.vector.tensor_copy(g_h[:, HID:AW], real[:, 0:1].to_broadcast([L, 2])))
                        nc.vector.tensor_scalar(g_h[:, 0:HID], g_hidden[:, :], 0.0, real[:, 0:1], ALU.max, ALU.mult).then_inc(s.g_h_ok, 1)
                        dve.wait_ge(s.g_sum_ps, i.i + 1)
                        nc.vector.tensor_copy(g_sum[:, :], sums_bank[0][:, 0:AW]).then_inc(s.g_sum_ok, 1)

                    run(dve, NE, tile_step, 1, [(0, NE - 1)])
                    run(dve, NTR, lambda t: [node_slot(at, t) for at in (2, 3, 5)], 2, [rounded(2, NTR, 2)])

                either(dve, windowed, general)

            @block.tensor
            def _(pe):
                pe.wait_ge(s.consts, 7)
                pe.wait_ge(s.w1a_in, 16)

                def node_step(q):
                    if q.within(NQ):
                        pe.wait_ge(s.h_ok, q.i + 1)
                        if q.least(2):
                            pe.wait_ge(s.hT_ok, q.i - 1)
                        for t in range(QUAD):
                            mm = nc.tensor.transpose(hT_bank[q.k % 2][:, t * L:(t + 1) * L], h_quad[:, q.k % 2, t, :], ident[:, :])
                        mm.then_inc(s.hT_ps, 1)
                    p = q.back(1)
                    if p.within(NQ):
                        pe.wait_ge(s.hT_ok, p.i + 1)
                        for half in range(2):
                            if p.least(2):
                                pe.wait_ge(s.P_ok, 2 * (p.i - 2) + half + 1)
                            for t in range(2):
                                mm = nc.tensor.matmul(P_bank[p.k % 2][half][:, t * HID:(t + 1) * HID],
                                                      hT[:, p.k % 2, (2 * half + t) * L:(2 * half + t + 1) * L], w1a[:, :],
                                                      start=True, stop=True)
                            mm.then_inc(s.P_ps, 1)
                    if q.turn is None and q.k == 5:
                        pe.wait_ge(s.faults_ok, 1)
                        nc.tensor.matmul(node_bank[1][:, 0:1], ones[:, :], faults[:, :], start=True, stop=True).then_inc(s.flag_ps, 1)

                run(pe, NQ + 1, node_step, 2, [rounded(6, NQ, 2)])

                pe.wait_ge(s.weights_in, 128)
                pe.wait_ge(s.wlo_ok, 1)
                pe.wait_ge(s.fills, 2)
                pe.wait_ge(s.hT_kept, NQ)
                pe.wait_ge(s.P_ok, 2 * NQ)

                def make_Q(g):
                    pe.wait_ge(hTw_sem[g.k % 2], 16 * g.uses(2))
                    nc.tensor.matmul(node_bank[1][:, 0:HID], hTw[:, g.k % 2, :], w1b[:, :], start=True, stop=True).then_inc(s.Qw_ps, 1)

                def node_slot(at, t):
                    if at == 0:
                        pe.wait_ge(S_sem[t.k % 2], 16 * t.uses(2))
                        if t.least(1):
                            pe.wait_ge(s.o_ok, t.i)
                        for k in range(2):
                            mm = nc.tensor.transpose(node_bank[0][:, k * L:(k + 1) * L], S_in[:, t.k % 2, k * L:(k + 1) * L], ident[:, :])
                        mm.then_inc(s.ST_ps, 1)
                    if at == 1:
                        pe.wait_ge(s.ST_ok, t.i + 1)
                        if t.least(1):
                            pe.wait_ge(s.U_ok, 2 * t.i)
                        for k in range(2):
                            mm = nc.tensor.matmul(node_bank[1][:, 0:D], ST[:, k * L:(k + 1) * L], w2[:, k, :], start=(k == 0), stop=(k == 1))
                        mm.then_inc(s.eff_ps, 1)
                    if at == 2:
                        pe.wait_ge(s.eff_ok, t.i + 1)
                        nc.tensor.transpose(node_bank[0][:, 0:L], eff[:, :], ident[:, :]).then_inc(s.effT_ps, 1)
                    if at == 3:
                        pe.wait_ge(s.effT_ok, t.i + 1)
                        for k in range(2):
                            o = node_bank[1][:, k * L:(k + 1) * L]
                            nc.tensor.matmul(o, u1[:, 0, k * L:(k + 1) * L], hT_all[:, t.span(L)], start=True, stop=False)
                            mm = nc.tensor.matmul(o, u1[:, 1, k * L:(k + 1) * L], effT[:, :], start=False, stop=True)
                        mm.then_inc(s.U_ps, 1)
                    if at == 4:
                        pe.wait_ge(s.U_ok, 2 * (t.i + 1))
                        for k in range(2):
                            mm = nc.tensor.matmul(node_bank[0][:, 0:D], U[:, k, :], u2[:, k, :], start=(k == 0), stop=(k == 1))
                        mm.then_inc(s.o_ps, 1)

                def edge_step(u):
                    if u.within(NU):
                        g, at = u.group(PAIRS), u.k % PAIRS
                        if at == 0:
                            pe.wait_ge(e_sem[g.k % 2], 16 * g.uses(2))
                        if u.least(2):
                            pe.wait_ge(s.elo_ok, u.i - 1)
                        for t in range(2):
                            mm = nc.tensor.transpose(eT_bank[u.k % 2][:, t * L:(t + 1) * L], e_in[:, g.k % 2, 2 * at + t, :], ident[:, :])
                        mm.then_inc(s.eT_ps, 1)
                    v = u.back(1)
                    if v.within(NU):
                        g, b = v.group(PAIRS), v.k % 2
                        pe.wait_ge(s.elo_ok, v.i + 1)
                        pe.wait_ge(s.ohT_ok, v.i + 1)
                        if v.k % PAIRS == 0:
                            pe.wait_ge(s.Qlo_ok, g.i + 1)
                        if v.least(2):
                            pe.wait_ge(s.pre_ok, v.i - 1)
                        for t in range(2):
                            o = pre_bank[b][:, t * HID:(t + 1) * HID]
                            of_tile = slice(t * L, (t + 1) * L)
                            nc.tensor.matmul(o, ehi[:, b, of_tile], whi[:, :], start=True, stop=False)
                            nc.tensor.matmul(o, ehi[:, b, of_tile], wlo[:, :], start=False, stop=False)
                            nc.tensor.matmul(o, elo[:, b, of_tile], whi[:, :], start=False, stop=False)
                            nc.tensor.matmul(o, ohT[:, b, t, :], Qhi[:, g.k % 2, :], start=False, stop=False)
                            mm = nc.tensor.matmul(o, ohT[:, b, t, :], Qlo[:, g.k % 2, :], start=False, stop=True)
                        mm.then_inc(s.pre_ps, 1)
                    g, at = u.group(PAIRS), u.k % PAIRS
                    t = g.back(LAG + 2)
                    if t.within(NTR):
                        if at == 1:
                            pe.wait_ge(s.Qlo_ok, g.i + 1 if g.within(NG) else NG)
                        node_slot(at, t)
                    if at == 4 and g.back(-1).within(NG):
                        if t.least(0):
                            pe.wait_ge(s.U_ok, 2 * (t.i + 1))
                        elif g.least(0):
                            pe.wait_ge(s.Qlo_ok, g.i + 1)
                        make_Q(g.back(-1))
                    w = u.back(3)
                    if w.within(NU):
                        g, at, b = w.group(PAIRS), w.k % PAIRS, w.k % 2
                        pe.wait_ge(s.lo_ok, w.i + 1)
                        pe.wait_ge(s.oh_ok, w.i + 1)
                        if at == 0 and g.least(2):
                            pe.wait_ge(s.win_ok, g.i - 1)
                        for t in range(2):
                            o = sums_bank[g.k % 2][:, 0:AW]
                            nc.tensor.matmul(o, oh[:, b, t, :], hhi[:, b, t, :], start=(at == 0 and t == 0), stop=False)
                            mm = nc.tensor.matmul(o, oh[:, b, t, :], hlo[:, b, t, :], start=False, stop=(at == PAIRS - 1 and t == 1))
                        mm.then_inc(s.sums_ps, 1)

                def windowed():
                    make_Q(Step(0))
                    run(pe, NSTEP * PAIRS, edge_step, UNROLL, EDGE_LOOPS)

                def general():
                    def Q_step(q):
                        pe.wait_ge(s.g_hT_ok, q.i + 1)
                        for half in range(2):
                            if q.least(1):
                                pe.wait_ge(s.g_Q_ok, 2 * (q.i - 1) + half + 1)
                            for t in range(2):
                                mm = nc.tensor.matmul(P_bank[0][half][:, t * HID:(t + 1) * HID],
                                                      g_hT[:, (2 * half + t) * L:(2 * half + t + 1) * L], w1b[:, :], start=True, stop=True)
                            mm.then_inc(s.g_Q_ps, 1)

                    run(pe, NQ, Q_step, 1, [(1, NQ)])
                    pe.wait_ge(s.g_Q_ok, 2 * NQ)

                    def tile_step(i):
                        pe.wait_ge(s.g_in, 64 * (i.i + 1))
                        nc.tensor.transpose(eT_bank[0][:, 0:L], g_e[:, :], ident[:, :]).then_inc(s.g_eT_ps, 1)
                        pe.wait_ge(s.g_eT_ok, i.i + 1)
                        nc.tensor.matmul(P_bank[0][0][:, 0:HID], g_eT[:, :], w1c[:, :], start=True, stop=True).then_inc(s.g_pre_ps, 1)
                        pe.wait_ge(s.g_h_ok, i.i + 1)
                        nc.tensor.matmul(sums_bank[0][:, 0:AW], g_same[:, :], g_h[:, :], start=True, stop=True).then_inc(s.g_sum_ps, 1)

                    run(pe, NE, tile_step, 1, [(0, NE)])
                    run(pe, NTR, lambda t: [node_slot(at, t) for at in range(5)], 2, [rounded(2, NTR, 2)])

                either(pe, windowed, general)


_INS = ["x", "src", "dst", "edge_attr_128", "L0_gnn_re_w1", "L0_gnn_re_b1", "L0_gnn_re_w2", "L0_gnn_re_b2",
        "L0_gnn_ea_w1", "L0_gnn_ea_b1", "L0_gnn_ea_w2", "L0_gnn_ea_b2"]


def kernel(**inputs):
    import numpy as _np
    import concourse.bacc as _bacc
    from concourse import mybir as _mybir
    from concourse.bass_utils import run_bass_kernel_spmd as _run

    nc = _bacc.Bacc("TRN2", target_bir_lowering=False, num_devices=1)
    arrays, args = {}, []
    for name in _INS:
        a = _np.ascontiguousarray(inputs[name])
        arrays[f"in_{name}"] = a
        args.append(nc.dram_tensor(f"in_{name}", a.shape, _mybir.dt.from_np(a.dtype), kind="ExternalInput").ap())
    shape = arrays["in_x"].shape
    args.append(nc.dram_tensor("out_x", shape, _mybir.dt.float32, kind="ExternalOutput").ap())
    bass_gnn_preln_layer_kernel(nc, *args)
    r = _run(nc, [arrays], core_ids=[0])
    return r.results[0]["out_x"]
```

```python
import concourse.bass as bass
from concourse import mybir
from contextlib import ExitStack


def bass_gnn_preln_layer_kernel(nc, x, src, dst, edge_attr, re_w1, re_b1, re_w2, re_b2,
                                ea_w1, ea_b1, ea_w2, ea_b2, out):
    f32, f32r = mybir.dt.float32, mybir.dt.float32r
    bf16, i32 = mybir.dt.bfloat16, mybir.dt.int32
    ALU = mybir.AluOpType
    ACT = mybir.ActivationFunctionType
    AX = mybir.AxisListType.X

    L = 128
    N, D = x.shape
    E = src.shape[0]
    HID = re_w1.shape[1]
    EPS = 1e-5

    QUAD = 4
    NQ = -(-N // (QUAD * L))
    NT = NQ * QUAD
    NPAD = NT * L
    FULL = N // L
    REST = N - FULL * L
    NTR = -(-N // L)
    XQ = [0, 2, 5, *range(10, NQ, 5), NQ]
    NXC = len(XQ) - 1

    TG = 14
    GE = TG * L
    NG = -(-E // GE)
    TAIL0 = E - GE
    OVER = NG * GE - E
    WIN = L
    PAIRS = TG // 2
    NU = NG * PAIRS
    AW = HID + 2
    DUMMY = NPAD
    NE = -(-E // L)
    GTAIL0 = E - L
    GOVER = NE * L - E
    OUTSIDE = -1000.0
    UNROLL = 2 * PAIRS

    LAG = 15
    AHEAD = 2
    NSTEP = NTR + LAG + 2
    NZ = max(NT + 1, NG + 4)

    P_dram = nc.dram_tensor("P_dram", [NPAD, HID], f32).ap()
    Q_dram = nc.dram_tensor("Q_dram", [NPAD, HID], f32).ap()
    sums_dram = nc.dram_tensor("sums_dram", [NZ * L, AW], f32).ap()
    local_dram = nc.dram_tensor("local_dram", [NG, GE], f32).ap()
    local_row_dram = nc.dram_tensor("local_row_dram", [NG, GE], bf16).ap()

    ctx = ExitStack()
    with ctx:
        def sb(name, shape, dt=f32):
            return ctx.enter_context(nc.sbuf_tensor(name, shape, dt))

        def sem(name):
            return ctx.enter_context(nc.semaphore(name))

        bank = [ctx.enter_context(nc.psum_tensor(f"bank{i}", [L, 512], f32)) for i in range(8)]

        w1a = sb("w1a", [L, HID])
        w1b = sb("w1b", [L, HID])
        w1c = sb("w1c", [L, HID])
        whi = sb("whi", [L, HID], f32r)
        wlo = sb("wlo", [L, HID], f32r)
        b1_all = sb("b1_all", [L, HID])
        w2 = sb("w2", [L, 2, D])
        b2_all = sb("b2_all", [L, D])
        u1 = sb("u1", [L, 2, HID])
        c1 = sb("c1", [L, 2])
        u2 = sb("u2", [L, 2, D])
        c2_all = sb("c2_all", [L, D])
        ident = sb("ident", [L, L])
        iota_free = sb("iota_free", [L, L])
        minus_part = sb("minus_part", [L, 1])
        pace = sb("pace", [L, 1])
        eps_col = sb("eps_col", [L, 1])
        one_col = sb("one_col", [L, 1])
        ones = sb("ones", [L, L])
        zeros = sb("zeros", [L, AW])
        flag = sb("flag", [L, 1], i32)

        x_all = sb("x_all", [L, NT, D])
        hT_all = sb("hT_all", [L, NPAD])

        AREA = 36 * 1024
        area = sb("area", [L, AREA // 4])

        class Lay:
            def __init__(self):
                self.at = 0

            def __call__(self, *shape, dt=f32):
                n = 1
                for extent in shape:
                    n *= extent
                words = -(-n * {f32: 4, i32: 4, bf16: 2}[dt] // 4)
                a = area[:, self.at:self.at + words]
                self.at += words
                assert self.at * 4 <= AREA
                if dt != f32:
                    a = a.bitcast(dt)
                if len(shape) == 2:
                    a = a.rearrange("p (a b) -> p a b", a=shape[0])
                if len(shape) == 3:
                    a = a.rearrange("p (a b c) -> p a b c", a=shape[0], b=shape[1])
                return a

        early = Lay()
        recv = early(GE, dt=i32)
        local = early(GE)
        local_row = early(GE, dt=bf16)
        first = early(1)
        lead = early(1)
        most = early(1)
        least = early(1)
        outside = early(4)
        faults = early(1)
        stats = early(2, QUAD * 6)
        mv = early(2, QUAD * 2)
        std = early(2, QUAD)
        rstd = early(2, QUAD)
        shift = early(2, QUAD)
        P_out = early(4, QUAD, HID)

        late = Lay()
        P_in = late(2, TG, HID)
        pre = late(2, 2, HID)

        e_in = sb("e_in", [L, 2, TG, D])
        of_stage1 = e_in[:, :, :, :].rearrange("p b t d -> p (b t d)")
        h_quad = of_stage1[:, 0:2 * QUAD * D].rearrange("p (b t d) -> p b t d", b=2, t=QUAD)
        hT = of_stage1[:, 2 * QUAD * D:2 * QUAD * D + 4 * QUAD * L].rearrange("p (b n) -> p b n", b=4)
        row = sb("row", [L, 2, GE], bf16)
        col = sb("col", [L, 2, TG])
        idx = sb("idx", [L, 4, TG], i32)
        hTw = sb("hTw", [L, 2, L])
        Qhi = sb("Qhi", [L, 2, HID], f32r)
        Qlo = sb("Qlo", [L, 2, HID], f32r)
        ehi = sb("ehi", [L, 2, 2 * L], f32r)
        elo = sb("elo", [L, 2, 2 * L], f32r)
        dist = sb("dist", [L, 2, 2 * L])
        ohT = sb("ohT", [L, 2, 2, L], f32r)
        oh = sb("oh", [L, 2, 2, L], f32r)
        hhi = sb("hhi", [L, 2, 2, AW], f32r)
        hlo = sb("hlo", [L, 2, 2, AW], f32r)
        win = sb("win", [L, AW])
        win_out = sb("win_out", [L, 2, AW])

        gen = Lay()
        g_src = gen(1, dt=i32)
        g_dst = gen(1, dt=i32)
        g_dst_row = gen(L, dt=i32)
        g_e = gen(D)
        g_P = gen(HID)
        g_Q = gen(HID)
        g_eT = gen(L)
        g_recv = gen(1)
        g_recv_row = gen(L)
        g_same = gen(L)
        g_earlier = gen(L)
        g_count = gen(1)
        g_again = gen(1)
        g_away = gen(1)
        g_row = gen(1, dt=i32)
        g_hidden = gen(HID)
        g_h = gen(AW)
        g_sum = gen(AW)
        below = gen(L)
        all_edges = gen(1)
        new_edges = gen(1)
        dummy_row = gen(1)
        g_hT = gen(QUAD * L)
        g_Q_out = gen(QUAD, HID)

        S_in = sb("S_in", [L, 2, AW])
        ST = sb("ST", [L, 2 * L])
        eff = sb("eff", [L, D])
        effT = sb("effT", [L, L])
        U = sb("U", [L, 2, L])
        o_out = sb("o_out", [L, 2, D])

        names = """c2_in w1a_in b1_in weights_in ident0 consts zeroed dst_in first_ok lead_ok local_ok range_ok outside_ok
            faults_ok flag_ps flag_ok tail_masked row_ok local_st x_pad x_rest_in whi_ok wlo_ok fills
            stat_ok agg_ok std_ok rstd_ok shift_ok h_ok hT_ps hT_ok hT_kept0 hT_kept1 hT_kept2 hT_kept3 x_biased P_ps P_ok P_st0 P_st1 P_st2 P_st3
            e_in0 e_in1 col_in0 col_in1 row_in0 row_in1 idx_in0 idx_in1 idx_in2 idx_in3 hTw_in0 hTw_in1
            zero_st0 zero_st1 zero_st2 zero_st3
            Qw_ps Qhi_ok Qlo_ok eT_ps ehi_ok elo_ok dist_ok ohT_ok pre_ps pre_ok hi_ok lo_ok oh_ok sums_ps
            win_in win_ok win_st
            S_in0 S_in1 ST_ps ST_ok eff_ps eff_ok effT_ps effT_ok U_ps U_ok o_ps o_ok o_st0 o_st1
            g_free g_zero_st g_hT_ok g_Q_ps g_Q_ok g_Q_st g_ready g_in g_pool g_masks g_rows g_chain g_eT_ps g_eT_ok
            g_pre_ps g_h_ok g_sum_ps g_sum_ok g_scattered""".split()
        s = type("Sems", (), {n: sem(n) for n in names})
        passed = {e: sem(f"passed_{n}") for n, e in (("pool", nc.gpsimd.engine), ("sp", nc.sync.engine), ("dve", nc.vector.engine))}
        gathered = [[sem(f"gathered{b}_{u}") for u in range(PAIRS)] for b in range(2)]
        x_in = [sem(f"x_in{c}") for c in range(NXC)]
        hT_kept = [s.hT_kept0, s.hT_kept1, s.hT_kept2, s.hT_kept3]
        P_st = [s.P_st0, s.P_st1, s.P_st2, s.P_st3]
        e_sem, col_sem, row_sem = [s.e_in0, s.e_in1], [s.col_in0, s.col_in1], [s.row_in0, s.row_in1]
        hTw_sem, idx_sem = [s.hTw_in0, s.hTw_in1], [s.idx_in0, s.idx_in1, s.idx_in2, s.idx_in3]
        zero_sem = [s.zero_st0, s.zero_st1, s.zero_st2, s.zero_st3]
        S_sem, o_st = [s.S_in0, s.S_in1], [s.o_st0, s.o_st1]

        hT_bank, P_bank = [bank[0], bank[3]], [bank[1:3], bank[4:6]]
        eT_bank, pre_bank, sums_bank = bank[0:2], bank[2:4], bank[4:6]
        node_bank = bank[6:8]

        P_rows = P_dram.rearrange("(q t p) c -> q p t c", t=QUAD, p=L)
        Q_rows = Q_dram.rearrange("(q t p) c -> q p t c", t=QUAD, p=L)
        x_rows = x[0:FULL * L, :].rearrange("(t p) d -> p t d", p=L)

        class Step:

            def __init__(self, k, turn=None, unroll=0, loops=1):
                self.k, self.turn, self.unroll, self.loops = k, turn, unroll, loops
                self.i = k if turn is None else turn * unroll + k
                self.last = k + (loops - 1) * unroll

            def back(self, n):
                return Step(self.k - n, self.turn, self.unroll, self.loops)

            def group(self, size, shift=0):
                return Step((self.k + shift) // size, self.turn, self.unroll // size, self.loops)

            def uses(self, buffers):
                return self.group(buffers).i + 1

            def within(self, n):
                inside = 0 <= self.k and self.last < n
                assert inside or self.last < 0 or self.k >= n, (self.k, self.last, n)
                return inside

            def least(self, n):
                assert self.k >= n or self.last < n, (self.k, self.last, n)
                return self.k >= n

            def span(self, size):
                return bass.ds(self.i * size, size)

        def run(eng, n, step, unroll=1, loops=(), first=0):
            k = first
            for a, b in (*loops, (n, n)):
                while k < a:
                    step(Step(k))
                    k += 1
                if b > a:
                    assert (b - a) % unroll == 0 and b <= n
                    with eng.Fori(0, (b - a) // unroll) as turn:
                        for at in range(unroll):
                            step(Step(a + at, turn, unroll, (b - a) // unroll))
                    k = b

        def rounded(a, b, unroll):
            return (a, a + max(0, b - a) // unroll * unroll)

        GROUP_LOOPS = [rounded(4, LAG + 2, 4), rounded(LAG + 5, NG - 1, 4)]
        EDGE_LOOPS = [rounded(4 * PAIRS, (LAG + 2) * PAIRS, UNROLL), rounded((LAG + 5) * PAIRS, (NG - 1) * PAIRS, UNROLL)]

        def apart(eng):
            eng.sem_inc(passed[eng.engine], 1)

        def either(eng, windowed, general):
            eng.wait_ge(s.flag_ok, 1)
            outsiders = eng.value_load(flag[0:1, 0:1], min_val=0, max_val=4 * NG)
            with eng.If(outsiders > 0):
                general()
            with eng.Else():
                windowed()

        with nc.Block() as block:

            @block.sync
            def _(sp):
                def load_x(c):
                    t0, t1 = XQ[c] * QUAD, min(XQ[c + 1] * QUAD, FULL)
                    sp.dma_start(x_all[:, t0:t1, :], x_rows[:, t0:t1, :]).then_inc(x_in[c], 16)

                load_x(0)
                sp.dma_start(recv[0:NG - 1, :], dst[0:(NG - 1) * GE].rearrange("(g e) -> g e", e=GE)).then_inc(s.dst_in, 16)
                sp.dma_start(recv[NG - 1:NG, :], dst[TAIL0:E].rearrange("(g e) -> g e", e=GE)).then_inc(s.dst_in, 16)
                for c in range(1, NXC):
                    load_x(c)
                sp.wait_ge(s.x_pad, 1)
                sp.dma_start(x_all[0:REST, FULL, :], x[FULL * L:N, :]).then_inc(s.x_rest_in, 16)

                for tile, source in ((w1b[:, :], re_w1[D:2 * D, :]), (w1c[:, :], re_w1[2 * D:3 * D, :]),
                                     (w2[:, :, :], re_w2.rearrange("(k p) n -> p k n", p=L)),
                                     (b2_all[:, :], re_b2.partition_broadcast(L)),
                                     (u1[:, :, :], ea_w1.rearrange("(k p) n -> p k n", p=L)),
                                     (u2[:, :, :], ea_w2.rearrange("(k p) n -> p k n", p=L))):
                    sp.dma_start(tile, source).then_inc(s.weights_in, 16)
                with nc.allow_non_contiguous_dma(reason="256 biases, two to a partition"):
                    sp.dma_start(c1[:, :], ea_b1.rearrange("(k p) -> p k", p=L)).then_inc(s.weights_in, 16)

                def keep(q):
                    sp.wait_ge(s.hT_ok, q.i + 1)
                    if q.turn is not None:
                        apart(sp)
                    sp.dma_start(hT_all[:, q.span(QUAD * L)], hT[:, q.k % 4, :]).then_inc(hT_kept[q.k % 4], 16)

                def store_P(q):
                    sp.wait_ge(s.P_ok, 2 * (q.i + 1))
                    if q.turn is not None:
                        apart(sp)
                    sp.dma_start(P_rows[bass.ds(q.i, 1)].rearrange("o p t c -> (o p) t c"),
                                 P_out[:, q.k % 4, :, :]).then_inc(P_st[q.k % 4], 16)

                def node_step(q):
                    if q.back(1).within(NQ):
                        store_P(q.back(1))
                    if q.within(NQ):
                        keep(q)
                    if q.turn is None and q.k == 10:
                        sp.wait_ge(s.tail_masked, 1)
                        sp.dma_start(local_dram, local[0:NG, :]).then_inc(s.local_st, 16)
                        sp.wait_ge(s.row_ok, 1)
                        sp.dma_start(local_row_dram, local_row[0:NG, :]).then_inc(s.local_st, 16)

                def edge_slice(g, size):
                    if g.turn is None:
                        e0 = TAIL0 if g.k == NG - 1 else g.k * GE
                        return slice(e0, e0 + size)
                    assert g.last < NG - 1
                    return bass.ds(g.i * GE, size)

                def load_idx(g):
                    if g.least(4):
                        sp.wait_ge(s.pre_ok, PAIRS * (g.i - 3))
                        apart(sp)
                    sp.dma_start(idx[:, g.k % 4, :], src[edge_slice(g, GE)].rearrange("(p t) -> p t", t=TG)).then_inc(idx_sem[g.k % 4], 16)

                load_idx(Step(0))
                load_idx(Step(1))
                run(sp, NQ + 1, node_step, 4, [rounded(2, 10, 4), rounded(11, NQ, 4)])

                def window(g):
                    return sp.value_load(dst[edge_slice(g, 1)].rearrange("(o n) -> o n", o=1), min_val=0, max_val=N - 1)

                def load_group(g):
                    b = g.k % 2
                    node = window(g)
                    if g.least(2):
                        sp.wait_ge(s.Qw_ps, g.i - 1)
                        apart(sp)
                    sp.dma_start(hTw[:, b, :], hT_all[:, bass.ds(node, WIN)]).then_inc(hTw_sem[b], 16)
                    if g.least(2):
                        sp.wait_ge(s.dist_ok, PAIRS * (g.i - 1))
                        apart(sp)
                    sp.dma_start(row[:, b, :], local_row_dram[bass.ds(g.i, 1), :].rearrange("o e -> (o e)").partition_broadcast(L)).then_inc(row_sem[b], 16)
                    if g.least(2):
                        sp.wait_ge(s.eT_ps, PAIRS * (g.i - 1))
                        apart(sp)
                    sp.dma_start(e_in[:, b, :, :], edge_attr[edge_slice(g, GE), :].rearrange("(p t) d -> p t d", t=TG)).then_inc(e_sem[b], 16)
                    if g.least(2):
                        sp.wait_ge(s.oh_ok, PAIRS * (g.i - 1))
                        apart(sp)
                    sp.dma_start(col[:, b, :], local_dram[bass.ds(g.i, 1), :].rearrange("o (p t) -> (o p) t", t=TG)).then_inc(col_sem[b], 16)

                def zero_tile(t):
                    sp.dma_start(sums_dram[t.span(L), :], zeros[:, :]).then_inc(zero_sem[t.k % 4], 16)

                def load_window(g, node, tiles):
                    if g.least(1):
                        sp.wait_ge(s.win_st, 16 * g.i)
                    for t in tiles:
                        if t.within(NZ):
                            sp.wait_ge(zero_sem[t.k % 4], 16 * t.uses(4))
                    if g.turn is not None:
                        apart(sp)
                    sp.dma_start(win[:, :], sums_dram[bass.ds(node, WIN), :]).then_inc(s.win_in, 16)

                def load_sums(t):
                    if t.least(2):
                        sp.wait_ge(s.eff_ok, t.i - 1)
                        apart(sp)
                    sp.dma_start(S_in[:, t.k % 2, :], sums_dram[t.span(L), :]).then_inc(S_sem[t.k % 2], 16)

                def store_out(t):
                    sp.wait_ge(s.o_ok, t.i + 1)
                    if t.turn is None and t.k == FULL:
                        sp.dma_start(out[FULL * L:N, :], o_out[0:REST, t.k % 2, :]).then_inc(o_st[t.k % 2], 16)
                    else:
                        assert t.last < FULL
                        apart(sp)
                        sp.dma_start(out[t.span(L), :], o_out[:, t.k % 2, :]).then_inc(o_st[t.k % 2], 16)

                def group_step(g):
                    if g.within(NG):
                        load_group(g)
                    if g.back(-2).within(NG):
                        load_idx(g.back(-2))
                    if g.back(-4).within(NZ):
                        zero_tile(g.back(-4))
                    stored = g.back(2)
                    if stored.within(NG):
                        node = window(stored)
                        node_after = window(g.back(1)) if g.back(1).within(NG) else None
                        sp.wait_ge(s.win_ok, stored.i + 1)
                        apart(sp)
                        sp.dma_start(sums_dram[bass.ds(node, WIN), :], win_out[:, stored.k % 2, :]).then_inc(s.win_st, 16)
                        if g.back(1).within(NG):
                            load_window(g.back(1), node_after, [g.back(-1)])
                        elif stored.k == NG - 1:
                            sp.wait_ge(s.win_st, 16 * NG)
                    t = g.back(LAG + 2)
                    if t.within(NTR):
                        load_sums(t)
                    if t.back(1).within(NTR):
                        store_out(t.back(1))

                def windowed():
                    sp.wait_ge(s.local_st, 32)
                    for b in range(4):
                        sp.wait_ge(hT_kept[b], 16 * ((NQ + 3 - b) // 4))
                    sp.wait_ge(s.zeroed, 1)
                    for t in range(4):
                        zero_tile(Step(t))
                    group_step(Step(0))
                    load_window(Step(0), window(Step(0)), [Step(t) for t in range(3)])
                    run(sp, NSTEP + 1, group_step, 4, GROUP_LOOPS, first=1)

                def general():
                    for b in range(4):
                        sp.wait_ge(P_st[b], 16 * ((NQ + 3 - b) // 4))
                    sp.wait_ge(s.local_st, 32)
                    sp.wait_ge(s.zeroed, 1)
                    sp.sem_inc(s.g_free, 1)
                    run(sp, NZ, lambda t: sp.dma_start(sums_dram[t.span(L), :], zeros[:, :]).then_inc(s.g_zero_st, 16), 1, [(0, NZ)])

                    def store_Q(q):
                        sp.wait_ge(s.g_Q_ok, 2 * (q.i + 1))
                        apart(sp)
                        sp.dma_start(Q_rows[bass.ds(q.i, 1)].rearrange("o p t c -> (o p) t c"), g_Q_out[:, :, :]).then_inc(s.g_Q_st, 16)

                    run(sp, NQ, store_Q, 1, [(0, NQ)])
                    sp.wait_ge(s.g_zero_st, 16 * NZ)
                    sp.wait_ge(s.g_Q_st, 16 * NQ)
                    sp.sem_inc(s.g_ready, 1)

                    def tile_step(i):
                        if i.least(1):
                            sp.wait_ge(s.g_scattered, 16 * i.i)
                            apart(sp)
                        e = bass.ds(GTAIL0, L) if i.turn is None and i.k == NE - 1 else i.span(L)
                        sp.dma_start(g_src[:, :], src[e].rearrange("(p o) -> p o", o=1)).then_inc(s.g_in, 16)
                        sp.dma_start(g_dst[:, :], dst[e].rearrange("(p o) -> p o", o=1)).then_inc(s.g_in, 16)
                        sp.dma_start(g_dst_row[:, :], dst[e].partition_broadcast(L)).then_inc(s.g_in, 16)
                        sp.dma_start(g_e[:, :], edge_attr[e, :]).then_inc(s.g_in, 16)

                    run(sp, NE, tile_step, 1, [(1, NE - 1)])
                    sp.wait_ge(s.g_scattered, 16 * NE)

                    def node_tile(t):
                        if t.within(NTR):
                            load_sums(t)
                        if t.back(1).within(NTR):
                            store_out(t.back(1))

                    run(sp, NTR + 1, node_tile, 2, [rounded(4, NTR - 1, 2)])

                either(sp, windowed, general)
                for b in range(2):
                    sp.wait_ge(o_st[b], 16 * ((NTR + 1 - b) // 2))

            @block.gpsimd
            def _(pool):
                nc.gpsimd.memset(x_all[:, FULL:NT, :], 0.0).then_inc(s.x_pad, 1)
                nc.gpsimd.memset(ident[:], 0.0).then_inc(s.ident0, 1)
                nc.gpsimd.memset(eps_col[:], EPS).then_inc(s.consts, 1)
                nc.gpsimd.memset(one_col[:], 1.0).then_inc(s.consts, 1)
                nc.gpsimd.memset(ones[:], 1.0).then_inc(s.consts, 1)
                pool.wait_ge(s.ident0, 1)
                nc.gpsimd.affine_select(out=ident[:], in_=ident[:], compare_op=ALU.not_equal, fill=1.0, base=0,
                                        pattern=[[-1, L]], channel_multiplier=1).then_inc(s.consts, 1)
                nc.gpsimd.iota(iota_free[:], pattern=[[1, L]], base=0, channel_multiplier=0,
                               allow_small_or_imprecise_dtypes=True).then_inc(s.consts, 1)
                nc.gpsimd.iota(minus_part[:], pattern=[[0, 1]], base=0, channel_multiplier=-1,
                               allow_small_or_imprecise_dtypes=True).then_inc(s.consts, 1)
                nc.gpsimd.iota(pace[:], pattern=[[0, 1]], base=0, channel_multiplier=L,
                               allow_small_or_imprecise_dtypes=True).then_inc(s.consts, 1)
                nc.gpsimd.memset(zeros[:], 0.0).then_inc(s.zeroed, 1)

                pool.wait_ge(s.c2_in, 16)

                def add_bias(q):
                    if q.turn is None and q.k == 5:
                        pool.wait_ge(s.range_ok, 2)
                        pool.wait_ge(s.consts, 7)
                        pool.wait_ge(s.zeroed, 1)
                        pool.wait_ge(s.x_biased, 5)
                        q0 = (NG - 1) // 32 * 32
                        nc.gpsimd.affine_select(out=local[q0:NG, 0:OVER], in_=local[q0:NG, 0:OVER], compare_op=ALU.not_equal,
                                                fill=OUTSIDE, base=q0 - (NG - 1), pattern=[[0, OVER]],
                                                channel_multiplier=1).then_inc(s.tail_masked, 1)
                        pool.wait_ge(s.tail_masked, 1)
                    pool.wait_ge(s.h_ok, q.i + 1)
                    nc.gpsimd.tensor_tensor(x_all[:, q.span(QUAD), :], x_all[:, q.span(QUAD), :],
                                            c2_all[:, :].unsqueeze(1).to_broadcast([L, QUAD, D]), ALU.add).then_inc(s.x_biased, 1)

                run(pool, NQ, add_bias, 1, [(6, NQ)])

                def windowed():
                    for b in range(4):
                        pool.wait_ge(P_st[b], 16 * ((NQ + 3 - b) // 4))
                    pool.wait_ge(s.local_st, 32)

                    def gather(g):
                        b = g.k % 2
                        pool.wait_ge(idx_sem[g.k % 4], 16 * g.uses(4))
                        apart(pool)
                        for u in range(PAIRS):
                            if g.least(2):
                                pool.wait_ge(s.pre_ok, PAIRS * (g.i - 2) + u + 1)
                                apart(pool)
                            for t in (2 * u, 2 * u + 1):
                                nc.gpsimd.indirect_dma_start(
                                    out=P_in[:, b, t, :], out_offset=None, in_=P_dram[:, :],
                                    in_offset=bass.IndirectOffsetOnAxis(ap=idx[:, g.k % 4, t:t + 1], axis=0)
                                ).then_inc(gathered[b][u], 16)

                    run(pool, NG, gather, 4, [rounded(4, NG, 4)])

                def general():
                    pool.wait_ge(s.g_free, 1)
                    nc.gpsimd.memset(below[:], 1.0).then_inc(s.g_pool, 1)
                    nc.gpsimd.memset(all_edges[:], 1.0).then_inc(s.g_masks, 1)
                    nc.gpsimd.memset(new_edges[:], 1.0).then_inc(s.g_pool, 1)
                    nc.gpsimd.iota(dummy_row[:], pattern=[[0, 1]], base=DUMMY, channel_multiplier=1,
                                   allow_small_or_imprecise_dtypes=True).then_inc(s.g_masks, 1)
                    pool.wait_ge(s.g_pool, 2)
                    nc.gpsimd.affine_select(out=below[:], in_=below[:], compare_op=ALU.is_ge, fill=0.0, base=-1,
                                            pattern=[[-1, L]], channel_multiplier=1).then_inc(s.g_masks, 1)
                    nc.gpsimd.affine_select(out=new_edges[:], in_=new_edges[:], compare_op=ALU.is_ge, fill=0.0, base=-GOVER,
                                            pattern=[[0, 1]], channel_multiplier=1).then_inc(s.g_masks, 1)
                    pool.wait_ge(s.g_ready, 1)

                    def tile_step(i):
                        pool.wait_ge(s.g_in, 64 * (i.i + 1))
                        apart(pool)
                        for rows, table, index in ((g_P, P_dram, g_src), (g_Q, Q_dram, g_dst)):
                            nc.gpsimd.indirect_dma_start(
                                out=rows[:, :], out_offset=None, in_=table[:, :],
                                in_offset=bass.IndirectOffsetOnAxis(ap=index[:, 0:1], axis=0)).then_inc(s.g_rows, 16)
                        pool.wait_ge(s.g_sum_ok, i.i + 1)
                        apart(pool)
                        nc.gpsimd.indirect_dma_start(
                            out=sums_dram[:, :], out_offset=bass.IndirectOffsetOnAxis(ap=g_row[:, 0:1], axis=0),
                            in_=g_sum[:, :], in_offset=None, compute_op=ALU.add).then_inc(s.g_scattered, 16)

                    run(pool, NE, tile_step, 1, [(0, NE)])

                either(pool, windowed, general)

            @block.scalar
            def _(act):
                act.dma_start(w1a[:, :], re_w1[0:D, :]).then_inc(s.w1a_in, 16)
                act.dma_start(b1_all[:, :], re_b1.partition_broadcast(L)).then_inc(s.b1_in, 16)
                act.dma_start(c2_all[:, :], ea_b2.partition_broadcast(L)).then_inc(s.c2_in, 16)
                act.wait_ge(s.consts, 7)

                def take_std(q):
                    act.wait_ge(s.agg_ok, QUAD * (q.i + 1))
                    if q.least(2):
                        act.wait_ge(s.rstd_ok, q.i - 1)
                    b = q.k % 2
                    nc.scalar.activation(std[:, b, :], mv[:, b, :].rearrange("p (t c) -> p t c", c=2)[:, :, 1],
                                         ACT.Sqrt, bias=eps_col[:, 0:1]).then_inc(s.std_ok, 1)

                def normalise(q):
                    act.wait_ge(s.shift_ok, q.i + 1)
                    if q.least(2):
                        act.wait_ge(s.hT_ps, q.i - 1)
                    for t in range(QUAD):
                        h = nc.scalar.activation(h_quad[:, q.k % 2, t, :], x_all[:, bass.ds(q.i * QUAD + t, 1), :].rearrange("p o d -> p (o d)"),
                                                 ACT.Relu, bias=shift[:, q.k % 2, t:t + 1], scale=rstd[:, q.k % 2, t:t + 1])
                    h.then_inc(s.h_ok, 1)

                take_std(Step(0))
                normalise(Step(0))
                take_std(Step(1))

                def node_step(q):
                    if q.back(-2).within(NQ):
                        take_std(q.back(-2))
                    if q.back(-1).within(NQ):
                        normalise(q.back(-1))
                    act.wait_ge(s.hT_ps, q.i + 1)
                    if q.least(4):
                        act.wait_ge(s.P_ps, 2 * (q.i - 3))
                        act.wait_ge(hT_kept[q.k % 4], 16 * (q.uses(4) - 1))
                    nc.scalar.copy(hT[:, q.k % 4, :], hT_bank[q.k % 2][:, :]).then_inc(s.hT_ok, 1)

                run(act, NQ, node_step, 4, [rounded(4, NQ - 2, 4)])

                act.wait_ge(s.weights_in, 112)
                nc.scalar.copy(whi[:, :], w1c[:, :]).then_inc(s.whi_ok, 1)

                def q_hi(g):
                    act.wait_ge(s.Qw_ps, g.i + 1)
                    if g.least(2):
                        act.wait_ge(s.pre_ps, PAIRS * (g.i - 1))
                    nc.scalar.copy(Qhi[:, g.k % 2, :], node_bank[1][:, 0:HID]).then_inc(s.Qhi_ok, 1)

                def take_distance(u):
                    g, at = u.group(PAIRS), u.k % PAIRS
                    if at == 0:
                        act.wait_ge(row_sem[g.k % 2], 16 * g.uses(2))
                    if u.least(2):
                        act.wait_ge(s.ohT_ok, u.i - 1)
                    nc.scalar.activation(dist[:, u.k % 2, :], row[:, g.k % 2, 2 * L * at:2 * L * (at + 1)],
                                         ACT.Abs, bias=minus_part[:, 0:1]).then_inc(s.dist_ok, 1)

                def node_slot(at, t):
                    if at == 0:
                        act.wait_ge(s.ST_ps, t.i + 1)
                        if t.least(1):
                            act.wait_ge(s.eff_ps, t.i)
                        nc.scalar.copy(ST[:, :], node_bank[0][:, 0:2 * L]).then_inc(s.ST_ok, 1)
                    if at == 2:
                        act.wait_ge(s.effT_ps, t.i + 1)
                        if t.least(1):
                            act.wait_ge(s.U_ps, 2 * t.i)
                        nc.scalar.copy(effT[:, :], node_bank[0][:, 0:L]).then_inc(s.effT_ok, 1)
                    if at in (4, 5):
                        k = at - 4
                        act.wait_ge(s.U_ps, 2 * t.i + k + 1)
                        if t.least(1):
                            act.wait_ge(s.o_ps, t.i)
                        nc.scalar.activation(U[:, k, :], node_bank[1][:, k * L:(k + 1) * L], ACT.Relu,
                                             bias=c1[:, k:k + 1]).then_inc(s.U_ok, 1)

                def edge_step(u):
                    g, at = u.group(PAIRS), u.k % PAIRS
                    if at == 4 and g.back(-1).within(NG):
                        q_hi(g.back(-1))
                    if u.within(NU):
                        act.wait_ge(s.eT_ps, u.i + 1)
                        if u.least(2):
                            act.wait_ge(s.pre_ps, u.i - 1)
                        nc.scalar.copy(ehi[:, u.k % 2, :], eT_bank[u.k % 2][:, 0:2 * L]).then_inc(s.ehi_ok, 1)
                    v = u.back(2)
                    if v.within(NU):
                        act.wait_ge(s.pre_ok, v.i + 1)
                        if v.least(2):
                            act.wait_ge(s.sums_ps, v.i - 1)
                        nc.scalar.activation(hhi[:, v.k % 2, :, 0:HID], pre[:, v.k % 2, :, :], ACT.Relu).then_inc(s.hi_ok, 1)
                    if u.within(NU):
                        act.wait_ge(s.dist_ok, u.i + 1)
                        nc.scalar.activation(ohT[:, u.k % 2, :, :].rearrange("p t e -> p (t e)"), dist[:, u.k % 2, :],
                                             ACT.Relu, bias=one_col[:, 0:1], scale=-1.0).then_inc(s.ohT_ok, 1)
                    if u.back(-1).within(NU):
                        take_distance(u.back(-1))
                    g, at = u.group(PAIRS), u.k % PAIRS
                    if g.back(LAG + 2).within(NTR):
                        node_slot(at - 1, g.back(LAG + 2))

                def windowed():
                    act.wait_ge(s.local_st, 32)
                    take_distance(Step(0))
                    q_hi(Step(0))
                    run(act, NSTEP * PAIRS, edge_step, UNROLL, EDGE_LOOPS)

                def general():
                    act.wait_ge(s.g_free, 1)
                    for b in range(4):
                        act.wait_ge(hT_kept[b], 16 * ((NQ + 3 - b) // 4))

                    def hT_step(q):
                        if q.least(1):
                            act.wait_ge(s.g_Q_ps, 2 * q.i)
                        nc.scalar.copy(g_hT[:, :], hT_all[:, q.span(QUAD * L)]).then_inc(s.g_hT_ok, 1)

                    run(act, NQ, hT_step, 1, [(1, NQ)])

                    def tile_step(i):
                        act.wait_ge(s.g_eT_ps, i.i + 1)
                        nc.scalar.copy(g_eT[:, :], eT_bank[0][:, 0:L]).then_inc(s.g_eT_ok, 1)

                    run(act, NE, tile_step, 1, [(0, NE)])
                    run(act, NTR, lambda t: [node_slot(at, t) for at in (0, 2, 4, 5)], 1, [(2, NTR)])

                either(act, windowed, general)

            @block.vector
            def _(dve):
                nc.vector.memset(outside[:], 0.0).then_inc(s.first_ok, 1)
                nc.vector.memset(hhi[:, :, :, HID:AW].bitcast(f32), 1.0).then_inc(s.fills, 1)
                nc.vector.memset(hlo[:, :, :, HID:AW].bitcast(f32), 0.0).then_inc(s.fills, 1)

                def count_locals():
                    dve.wait_ge(s.dst_in, 32)
                    nc.vector.tensor_copy(first[0:NG, :], recv[0:NG, 0:1]).then_inc(s.first_ok, 1)
                    dve.wait_ge(s.first_ok, 2)
                    nc.vector.tensor_scalar(local[0:NG, :], recv[0:NG, :], first[0:NG, 0:1], None, ALU.subtract).then_inc(s.local_ok, 1)
                    dve.wait_ge(s.consts, 7)
                    nc.vector.tensor_tensor(lead[0:NG, :], first[0:NG, :], pace[0:NG, :], ALU.subtract).then_inc(s.lead_ok, 1)

                def take_range():
                    dve.wait_ge(s.local_ok, 1)
                    nc.vector.tensor_reduce(most[0:NG, :], local[0:NG, :], AX, ALU.max).then_inc(s.range_ok, 1)
                    nc.vector.tensor_reduce(least[0:NG, :], local[0:NG, :], AX, ALU.min).then_inc(s.range_ok, 1)

                def find_faults():
                    dve.wait_ge(s.range_ok, 2)
                    dve.wait_ge(s.lead_ok, 1)
                    nc.vector.tensor_scalar(outside[0:NG, 0:1], most[0:NG, :], float(WIN - 1), None, ALU.is_gt).then_inc(s.outside_ok, 1)
                    nc.vector.tensor_scalar(outside[0:NG, 1:2], least[0:NG, :], 0.0, None, ALU.is_lt).then_inc(s.outside_ok, 1)
                    nc.vector.tensor_scalar(outside[0:NG, 2:3], least[0:NG, :], lead[0:NG, 0:1], float(-LAG * L),
                                            ALU.add, ALU.is_lt).then_inc(s.outside_ok, 1)
                    nc.vector.tensor_scalar(outside[0:NG, 3:4], most[0:NG, :], lead[0:NG, 0:1], float(AHEAD * L - 1),
                                            ALU.add, ALU.is_gt).then_inc(s.outside_ok, 1)
                    dve.wait_ge(s.outside_ok, 4)
                    nc.vector.tensor_reduce(faults[:, :], outside[:, :], AX, ALU.add).then_inc(s.faults_ok, 1)

                def turn_rows():
                    dve.wait_ge(s.tail_masked, 1)
                    nc.vector.tensor_copy(local_row[0:NG, :].rearrange("g (t p) -> g p t", p=L),
                                          local[0:NG, :].rearrange("g (p t) -> g p t", t=TG)).then_inc(s.row_ok, 1)
                    dve.wait_ge(s.flag_ps, 1)
                    nc.vector.tensor_copy(flag[:, :], node_bank[1][:, 0:1]).then_inc(s.flag_ok, 1)

                def take_stats(q):
                    b = q.k % 2
                    if q.turn is None and q.k in XQ[:-1]:
                        dve.wait_ge(x_in[XQ.index(q.k)], 16)
                        if q.k == XQ[-2]:
                            dve.wait_ge(s.x_rest_in, 16)
                    if q.least(2):
                        dve.wait_ge(s.std_ok, q.i - 1)
                        dve.wait_ge(s.shift_ok, q.i - 1)
                    for t in range(QUAD):
                        nc.vector.bn_stats(stats[:, b, 6 * t:6 * t + 6],
                                           x_all[:, bass.ds(q.i * QUAD + t, 1), :].rearrange("p o d -> p (o d)")).then_inc(s.stat_ok, 1)

                def aggregate(q):
                    b = q.k % 2
                    dve.wait_ge(s.stat_ok, QUAD * (q.i + 1))
                    if q.turn is not None:
                        apart(dve)
                    for t in range(QUAD):
                        nc.vector.bn_aggr(mv[:, b, 2 * t:2 * t + 2], stats[:, b, 6 * t:6 * t + 6]).then_inc(s.agg_ok, 1)

                def invert_std(q):
                    dve.wait_ge(s.std_ok, q.i + 1)
                    if q.least(2):
                        dve.wait_ge(s.h_ok, q.i - 1)
                    nc.vector.reciprocal(rstd[:, q.k % 2, :], std[:, q.k % 2, :]).then_inc(s.rstd_ok, 1)

                def take_shift(q):
                    b = q.k % 2
                    dve.wait_ge(s.rstd_ok, q.i + 1)
                    nc.vector.scalar_tensor_tensor(shift[:, b, :], mv[:, b, :].rearrange("p (t c) -> p t c", c=2)[:, :, 0],
                                                   -1.0, rstd[:, b, :], ALU.mult, ALU.mult).then_inc(s.shift_ok, 1)

                def take_P(q, half):
                    dve.wait_ge(s.P_ps, 2 * q.i + half + 1)
                    if half == 0 and q.least(4):
                        dve.wait_ge(P_st[q.k % 4], 16 * (q.uses(4) - 1))
                    nc.vector.tensor_tensor(P_out[:, q.k % 4, 2 * half:2 * half + 2, :],
                                            P_bank[q.k % 2][half][:, :].rearrange("p (t c) -> p t c", t=2),
                                            b1_all[:, :].unsqueeze(1).to_broadcast([L, 2, HID]), ALU.add).then_inc(s.P_ok, 1)

                take_stats(Step(0))
                aggregate(Step(0))
                invert_std(Step(0))
                take_shift(Step(0))
                for q in (1, 2):
                    take_stats(Step(q))
                    aggregate(Step(q))
                dve.wait_ge(s.b1_in, 16)

                stage0 = {0: count_locals, 1: take_range, 2: find_faults, 7: turn_rows}

                def node_step(q):
                    if q.back(-1).within(NQ):
                        invert_std(q.back(-1))
                    if q.back(2).within(NQ):
                        take_P(q.back(2), 0)
                    if q.back(-1).within(NQ):
                        take_shift(q.back(-1))
                    if q.back(-3).within(NQ):
                        take_stats(q.back(-3))
                    if q.back(2).within(NQ):
                        take_P(q.back(2), 1)
                    if q.back(-3).within(NQ):
                        aggregate(q.back(-3))
                    if q.turn is None and q.k in stage0:
                        stage0[q.k]()

                run(dve, NQ + 2, node_step, 4, [rounded(a - 2, b - 3, 4) for a, b in zip(XQ[2:], XQ[3:])])

                dve.wait_ge(s.x_biased, NQ)
                dve.wait_ge(s.weights_in, 112)
                dve.wait_ge(s.whi_ok, 1)
                nc.vector.tensor_tensor(wlo[:, :], w1c[:, :], whi[:, :].bitcast(f32), ALU.subtract).then_inc(s.wlo_ok, 1)

                def q_lo(g):
                    dve.wait_ge(s.Qhi_ok, g.i + 1)
                    if g.least(2):
                        dve.wait_ge(s.pre_ps, PAIRS * (g.i - 1))
                    nc.vector.tensor_tensor(Qlo[:, g.k % 2, :], node_bank[1][:, 0:HID], Qhi[:, g.k % 2, :].bitcast(f32), ALU.subtract).then_inc(s.Qlo_ok, 1)

                def take_effects(t):
                        dve.wait_ge(s.eff_ps, t.i + 1)
                        if t.least(1):
                            dve.wait_ge(s.effT_ps, t.i)
                        nc.vector.scalar_tensor_tensor(eff[:, :], b2_all[:, :], S_in[:, t.k % 2, HID:HID + 1],
                                                       node_bank[1][:, 0:D], ALU.mult, ALU.add).then_inc(s.eff_ok, 1)

                def finish_tile(t):
                    dve.wait_ge(s.o_ps, t.i + 1)
                    if t.least(2):
                        dve.wait_ge(o_st[t.k % 2], 16 * (t.uses(2) - 1))
                    nc.vector.tensor_tensor(o_out[:, t.k % 2, :], node_bank[0][:, 0:D],
                                            x_all[:, bass.ds(t.i, 1), :].rearrange("p o d -> p (o d)"), ALU.add).then_inc(s.o_ok, 1)

                def edge_step(u):
                    v = u.back(2)
                    if v.within(NU):
                        g, b, at = v.group(PAIRS), v.k % 2, v.k % PAIRS
                        dve.wait_ge(s.pre_ps, v.i + 1)
                        dve.wait_ge(gathered[g.k % 2][at], 32 * g.uses(2))
                        if v.least(2):
                            dve.wait_ge(s.lo_ok, v.i - 1)
                        nc.vector.tensor_tensor(pre[:, b, :, :], pre_bank[b][:, :].rearrange("p (t c) -> p t c", t=2),
                                                P_in[:, g.k % 2, 2 * at:2 * at + 2, :], ALU.add).then_inc(s.pre_ok, 1)
                    g, at = u.group(PAIRS), u.k % PAIRS
                    if at == 1 and g.back(LAG + 3).within(NTR):
                        finish_tile(g.back(LAG + 3))
                    if at == 3 and g.back(LAG + 2).within(NTR):
                        take_effects(g.back(LAG + 2))
                    w = u.back(3)
                    if w.within(NU):
                        b = w.k % 2
                        dve.wait_ge(s.hi_ok, w.i + 1)
                        if w.least(2):
                            dve.wait_ge(s.sums_ps, w.i - 1)
                        nc.vector.scalar_tensor_tensor(hlo[:, b, :, 0:HID], pre[:, b, :, :], 0.0,
                                                       hhi[:, b, :, 0:HID].bitcast(f32), ALU.max, ALU.subtract).then_inc(s.lo_ok, 1)
                    if u.within(NU):
                        dve.wait_ge(s.ehi_ok, u.i + 1)
                        if u.least(2):
                            dve.wait_ge(s.pre_ps, u.i - 1)
                        nc.vector.tensor_tensor(elo[:, u.k % 2, :], eT_bank[u.k % 2][:, 0:2 * L], ehi[:, u.k % 2, :].bitcast(f32),
                                                ALU.subtract).then_inc(s.elo_ok, 1)
                    if v.within(NU):
                        g, at = v.group(PAIRS), v.k % PAIRS
                        if at == 0:
                            dve.wait_ge(col_sem[g.k % 2], 16 * g.uses(2))
                        if v.least(2):
                            dve.wait_ge(s.sums_ps, v.i - 1)
                        nc.vector.tensor_tensor(oh[:, v.k % 2, :, :], iota_free[:, :].unsqueeze(1).to_broadcast([L, 2, L]),
                                                col[:, g.k % 2, 2 * at:2 * at + 2].unsqueeze(2).to_broadcast([L, 2, L]),
                                                ALU.is_equal).then_inc(s.oh_ok, 1)
                    g, at = u.group(PAIRS), u.k % PAIRS
                    if at == 4 and g.back(-1).within(NG):
                        q_lo(g.back(-1))
                    if at == 4 and g.back(1).within(NG):
                        w = g.back(1)
                        dve.wait_ge(s.sums_ps, PAIRS * (w.i + 1))
                        dve.wait_ge(s.win_in, 16 * (w.i + 1))
                        if w.least(2):
                            dve.wait_ge(s.win_st, 16 * (w.i - 1))
                        nc.vector.tensor_tensor(win_out[:, w.k % 2, :], sums_bank[w.k % 2][:, 0:AW], win[:, :], ALU.add).then_inc(s.win_ok, 1)

                def windowed():
                    q_lo(Step(0))
                    run(dve, NSTEP * PAIRS + 2, edge_step, UNROLL, EDGE_LOOPS)

                def general():
                    dve.wait_ge(s.g_free, 1)

                    def Q_step(q):
                        if q.least(1):
                            dve.wait_ge(s.g_Q_st, 16 * q.i)
                        for half in range(2):
                            dve.wait_ge(s.g_Q_ps, 2 * q.i + half + 1)
                            nc.vector.tensor_copy(g_Q_out[:, 2 * half:2 * half + 2, :],
                                                  P_bank[0][half][:, :].rearrange("p (t c) -> p t c", t=2)).then_inc(s.g_Q_ok, 1)

                    run(dve, NQ, Q_step, 1, [(1, NQ)])
                    dve.wait_ge(s.g_masks, 4)
                    LINKS = 11

                    def tile_step(i):
                        linked = [0]

                        def link(ins):
                            linked[0] += 1
                            ins.then_inc(s.g_chain, 1)
                            dve.wait_ge(s.g_chain, i.i * LINKS + linked[0])

                        dve.wait_ge(s.g_in, 64 * (i.i + 1))
                        link(nc.vector.tensor_copy(g_recv[:, :], g_dst[:, :]))
                        link(nc.vector.tensor_copy(g_recv_row[:, :], g_dst_row[:, :]))
                        link(nc.vector.tensor_scalar(g_same[:, :], g_recv_row[:, :], g_recv[:, 0:1], None, ALU.is_equal))
                        link(nc.vector.tensor_tensor(g_earlier[:, :], g_same[:, :], below[:, :], ALU.mult))
                        link(nc.vector.tensor_reduce(g_count[:, :], g_earlier[:, :], AX, ALU.add))
                        link(nc.vector.tensor_scalar(g_again[:, :], g_count[:, :], 1.0, None, ALU.min))
                        link(nc.vector.tensor_tensor(g_away[:, :], dummy_row[:, :], g_recv[:, :], ALU.subtract))
                        link(nc.vector.scalar_tensor_tensor(g_row[:, :], g_away[:, :], g_again[:, 0:1], g_recv[:, :],
                                                            ALU.mult, ALU.add))
                        real = new_edges if i.turn is None and i.k == NE - 1 else all_edges
                        dve.wait_ge(s.g_pre_ps, i.i + 1)
                        dve.wait_ge(s.g_rows, 32 * (i.i + 1))
                        link(nc.vector.tensor_tensor(g_hidden[:, :], P_bank[0][0][:, 0:HID], g_P[:, :], ALU.add))
                        link(nc.vector.tensor_tensor(g_hidden[:, :], g_hidden[:, :], g_Q[:, :], ALU.add))
                        link(nc.vector.tensor_copy(g_h[:, HID:AW], real[:, 0:1].to_broadcast([L, 2])))
                        nc.vector.tensor_scalar(g_h[:, 0:HID], g_hidden[:, :], 0.0, real[:, 0:1], ALU.max, ALU.mult).then_inc(s.g_h_ok, 1)
                        dve.wait_ge(s.g_sum_ps, i.i + 1)
                        nc.vector.tensor_copy(g_sum[:, :], sums_bank[0][:, 0:AW]).then_inc(s.g_sum_ok, 1)

                    run(dve, NE, tile_step, 1, [(0, NE - 1)])
                    run(dve, NTR, lambda t: [take_effects(t), finish_tile(t)], 2, [rounded(2, NTR, 2)])

                either(dve, windowed, general)

            @block.tensor
            def _(pe):
                pe.wait_ge(s.consts, 7)
                pe.wait_ge(s.w1a_in, 16)

                def node_step(q):
                    if q.within(NQ):
                        pe.wait_ge(s.h_ok, q.i + 1)
                        if q.least(2):
                            pe.wait_ge(s.hT_ok, q.i - 1)
                        for t in range(QUAD):
                            mm = nc.tensor.transpose(hT_bank[q.k % 2][:, t * L:(t + 1) * L], h_quad[:, q.k % 2, t, :], ident[:, :])
                        mm.then_inc(s.hT_ps, 1)
                    p = q.back(1)
                    if p.within(NQ):
                        pe.wait_ge(s.hT_ok, p.i + 1)
                        for half in range(2):
                            if p.least(2):
                                pe.wait_ge(s.P_ok, 2 * (p.i - 2) + half + 1)
                            for t in range(2):
                                mm = nc.tensor.matmul(P_bank[p.k % 2][half][:, t * HID:(t + 1) * HID],
                                                      hT[:, p.k % 4, (2 * half + t) * L:(2 * half + t + 1) * L], w1a[:, :],
                                                      start=True, stop=True)
                            mm.then_inc(s.P_ps, 1)
                    if q.turn is None and q.k == 5:
                        pe.wait_ge(s.faults_ok, 1)
                        nc.tensor.matmul(node_bank[1][:, 0:1], ones[:, :], faults[:, :], start=True, stop=True).then_inc(s.flag_ps, 1)

                run(pe, NQ + 1, node_step, 4, [rounded(6, NQ, 4)])

                pe.wait_ge(s.weights_in, 112)
                pe.wait_ge(s.wlo_ok, 1)
                pe.wait_ge(s.fills, 2)
                for b in range(4):
                    pe.wait_ge(hT_kept[b], 16 * ((NQ + 3 - b) // 4))
                pe.wait_ge(s.P_ok, 2 * NQ)

                def make_Q(g):
                    pe.wait_ge(hTw_sem[g.k % 2], 16 * g.uses(2))
                    nc.tensor.matmul(node_bank[1][:, 0:HID], hTw[:, g.k % 2, :], w1b[:, :], start=True, stop=True).then_inc(s.Qw_ps, 1)

                def node_slot(at, t):
                    if at == 0:
                        pe.wait_ge(S_sem[t.k % 2], 16 * t.uses(2))
                        if t.least(1):
                            pe.wait_ge(s.o_ok, t.i)
                        for k in range(2):
                            mm = nc.tensor.transpose(node_bank[0][:, k * L:(k + 1) * L], S_in[:, t.k % 2, k * L:(k + 1) * L], ident[:, :])
                        mm.then_inc(s.ST_ps, 1)
                    if at == 1:
                        pe.wait_ge(s.ST_ok, t.i + 1)
                        if t.least(1):
                            pe.wait_ge(s.U_ok, 2 * t.i)
                        for k in range(2):
                            mm = nc.tensor.matmul(node_bank[1][:, 0:D], ST[:, k * L:(k + 1) * L], w2[:, k, :], start=(k == 0), stop=(k == 1))
                        mm.then_inc(s.eff_ps, 1)
                    if at == 2:
                        pe.wait_ge(s.eff_ok, t.i + 1)
                        nc.tensor.transpose(node_bank[0][:, 0:L], eff[:, :], ident[:, :]).then_inc(s.effT_ps, 1)
                    if at in (4, 5):
                        k = at - 4
                        if k == 0:
                            pe.wait_ge(s.effT_ok, t.i + 1)
                        else:
                            pe.wait_ge(s.U_ok, 2 * t.i + 1)
                        o = node_bank[1][:, k * L:(k + 1) * L]
                        nc.tensor.matmul(o, u1[:, 0, k * L:(k + 1) * L], hT_all[:, t.span(L)], start=True, stop=False)
                        nc.tensor.matmul(o, u1[:, 1, k * L:(k + 1) * L], effT[:, :], start=False, stop=True).then_inc(s.U_ps, 1)
                    if at == 6:
                        pe.wait_ge(s.U_ok, 2 * (t.i + 1))
                        for k in range(2):
                            mm = nc.tensor.matmul(node_bank[0][:, 0:D], U[:, k, :], u2[:, k, :], start=(k == 0), stop=(k == 1))
                        mm.then_inc(s.o_ps, 1)

                def transpose_features(u):
                    g, at = u.group(PAIRS), u.k % PAIRS
                    if at == 0:
                        pe.wait_ge(e_sem[g.k % 2], 16 * g.uses(2))
                    if u.least(2):
                        pe.wait_ge(s.elo_ok, u.i - 1)
                    for t in range(2):
                        mm = nc.tensor.transpose(eT_bank[u.k % 2][:, t * L:(t + 1) * L], e_in[:, g.k % 2, 2 * at + t, :], ident[:, :])
                    mm.then_inc(s.eT_ps, 1)

                def edge_step(u):
                    if u.back(-1).within(NU):
                        transpose_features(u.back(-1))
                    v = u.back(1)
                    if v.within(NU):
                        g, b = v.group(PAIRS), v.k % 2
                        pe.wait_ge(s.elo_ok, v.i + 1)
                        pe.wait_ge(s.ohT_ok, v.i + 1)
                        if v.k % PAIRS == 0:
                            pe.wait_ge(s.Qlo_ok, g.i + 1)
                        if v.least(2):
                            pe.wait_ge(s.pre_ok, v.i - 1)
                        for t in range(2):
                            o = pre_bank[b][:, t * HID:(t + 1) * HID]
                            of_tile = slice(t * L, (t + 1) * L)
                            nc.tensor.matmul(o, ehi[:, b, of_tile], whi[:, :], start=True, stop=False)
                            nc.tensor.matmul(o, ehi[:, b, of_tile], wlo[:, :], start=False, stop=False)
                            nc.tensor.matmul(o, elo[:, b, of_tile], whi[:, :], start=False, stop=False)
                            nc.tensor.matmul(o, ohT[:, b, t, :], Qhi[:, g.k % 2, :], start=False, stop=False)
                            mm = nc.tensor.matmul(o, ohT[:, b, t, :], Qlo[:, g.k % 2, :], start=False, stop=True)
                        mm.then_inc(s.pre_ps, 1)
                    g, at = u.group(PAIRS), u.k % PAIRS
                    t = g.back(LAG + 2)
                    if t.within(NTR):
                        if at == 2 and not t.least(1):
                            pe.wait_ge(s.Qlo_ok, g.i + 1)
                        if at == 5:
                            pe.wait_ge(s.Qlo_ok, min(g.i + 2, NG) if g.turn is None else g.i + 2)
                        node_slot(at - 1, t)
                    if at == 0 and t.back(1).within(NTR):
                        node_slot(6, t.back(1))
                    if at == 3 and g.back(-1).within(NG):
                        if t.least(0):
                            pe.wait_ge(s.eff_ok, t.i + 1)
                        else:
                            pe.wait_ge(s.Qlo_ok, g.i + 1)
                        make_Q(g.back(-1))
                    w = u.back(3)
                    if w.within(NU):
                        g, at, b = w.group(PAIRS), w.k % PAIRS, w.k % 2
                        pe.wait_ge(s.lo_ok, w.i + 1)
                        pe.wait_ge(s.oh_ok, w.i + 1)
                        if at == 0 and g.least(2):
                            pe.wait_ge(s.win_ok, g.i - 1)
                        for t in range(2):
                            o = sums_bank[g.k % 2][:, 0:AW]
                            nc.tensor.matmul(o, oh[:, b, t, :], hhi[:, b, t, :], start=(at == 0 and t == 0), stop=False)
                            mm = nc.tensor.matmul(o, oh[:, b, t, :], hlo[:, b, t, :], start=False, stop=(at == PAIRS - 1 and t == 1))
                        mm.then_inc(s.sums_ps, 1)

                def windowed():
                    make_Q(Step(0))
                    transpose_features(Step(0))
                    run(pe, NSTEP * PAIRS + 1, edge_step, UNROLL, EDGE_LOOPS)

                def general():
                    def Q_step(q):
                        pe.wait_ge(s.g_hT_ok, q.i + 1)
                        for half in range(2):
                            if q.least(1):
                                pe.wait_ge(s.g_Q_ok, 2 * (q.i - 1) + half + 1)
                            for t in range(2):
                                mm = nc.tensor.matmul(P_bank[0][half][:, t * HID:(t + 1) * HID],
                                                      g_hT[:, (2 * half + t) * L:(2 * half + t + 1) * L], w1b[:, :], start=True, stop=True)
                            mm.then_inc(s.g_Q_ps, 1)

                    run(pe, NQ, Q_step, 1, [(1, NQ)])
                    pe.wait_ge(s.g_Q_ok, 2 * NQ)

                    def tile_step(i):
                        pe.wait_ge(s.g_in, 64 * (i.i + 1))
                        nc.tensor.transpose(eT_bank[0][:, 0:L], g_e[:, :], ident[:, :]).then_inc(s.g_eT_ps, 1)
                        pe.wait_ge(s.g_eT_ok, i.i + 1)
                        nc.tensor.matmul(P_bank[0][0][:, 0:HID], g_eT[:, :], w1c[:, :], start=True, stop=True).then_inc(s.g_pre_ps, 1)
                        pe.wait_ge(s.g_h_ok, i.i + 1)
                        nc.tensor.matmul(sums_bank[0][:, 0:AW], g_same[:, :], g_h[:, :], start=True, stop=True).then_inc(s.g_sum_ps, 1)

                    run(pe, NE, tile_step, 1, [(0, NE)])
                    run(pe, NTR, lambda t: [node_slot(at, t) for at in range(7)], 2, [rounded(2, NTR, 2)])

                either(pe, windowed, general)


_INS = ["x", "src", "dst", "edge_attr_128", "L0_gnn_re_w1", "L0_gnn_re_b1", "L0_gnn_re_w2", "L0_gnn_re_b2",
        "L0_gnn_ea_w1", "L0_gnn_ea_b1", "L0_gnn_ea_w2", "L0_gnn_ea_b2"]


def kernel(**inputs):
    import numpy as _np
    import concourse.bacc as _bacc
    from concourse import mybir as _mybir
    from concourse.bass_utils import run_bass_kernel_spmd as _run

    nc = _bacc.Bacc("TRN2", target_bir_lowering=False, num_devices=1)
    arrays, args = {}, []
    for name in _INS:
        a = _np.ascontiguousarray(inputs[name])
        arrays[f"in_{name}"] = a
        args.append(nc.dram_tensor(f"in_{name}", a.shape, _mybir.dt.from_np(a.dtype), kind="ExternalInput").ap())
    shape = arrays["in_x"].shape
    args.append(nc.dram_tensor("out_x", shape, _mybir.dt.float32, kind="ExternalOutput").ap())
    bass_gnn_preln_layer_kernel(nc, *args)
    r = _run(nc, [arrays], core_ids=[0])
    return r.results[0]["out_x"]
```
